# Optimizing a Trainium2 kernel written in Bass

```python
import numpy as np
import jax
import jax.numpy as jnp

def _softmax(x, axis=-1):
    return jax.nn.softmax(x, axis=axis)

def _gelu(x):
    return jax.nn.gelu(x, approximate=True)

def _silu(x):
    return jax.nn.silu(x)

def _sigmoid(x):
    return jax.nn.sigmoid(x)

def _layernorm(x, axis=-1, eps=1e-05):
    m = jnp.mean(x, axis=axis, keepdims=True)
    v = jnp.var(x, axis=axis, keepdims=True)
    return (x - m) / jnp.sqrt(v + eps)

def _scatter_add(tgt, idx, src, axis=0):
    return tgt.at[idx].add(src)

def _segment_sum(src, seg, n):
    return jax.ops.segment_sum(src, seg, n)
kernel_name = 'mk_adj_resnorm_d2_adj_r2_d1f286'

def setup_inputs(seed: int=0):
    np.random.seed(seed)
    _w = jnp.asarray

    def _rec_inputs():
        import jax
        import jax.numpy as jnp
        _gk = jax.random.key(seed)
        x = -7.109e-05 + 0.9999 * jax.random.normal(jax.random.fold_in(_gk, 1), (128, 64, 256), jnp.float32)
        _w = (1.0 + jnp.arange(64, dtype=jnp.float32)) ** (-0.5)
        _w = _w / _w.mean()
        _pij = jnp.clip(0.0625 * _w[:, None] * _w[None, :], 0.0, 1.0)
        _a = jax.random.uniform(jax.random.fold_in(_gk, 2), (128, 64, 64)) < _pij
        adj = _a
        return (x, adj)
    x, adj = _rec_inputs()

    def _L0_gnn_setup():
        import jax, jax.numpy as jnp
        import numpy as np
        B, S, D, H = (1024, 64, 256, 8)
        HD = D // H
        SCALE = float(1.0 / np.sqrt(HD))

        def _static_masks():
            sq = np.arange(64)
            r = sq // 8
            f = sq % 8
            ri, rj = (r[:, None], r[None, :])
            fi, fj = (f[:, None], f[None, :])
            dr = np.abs(ri - rj)
            df = np.abs(fi - fj)
            eye = np.eye(64, dtype=bool)
            file_m = fi == fj
            rank_m = ri == rj
            diag_m = ri - fi == rj - fj
            adiag_m = ri + fi == rj + fj
            knight_m = (dr == 2) & (df == 1) | (dr == 1) & (df == 2) | eye
            king_m = (dr <= 1) & (df <= 1)
            return np.stack([file_m, rank_m, diag_m, adiag_m, knight_m, king_m])
        STATIC = jnp.asarray(_static_masks())
        EYE = jnp.eye(S, dtype=bool)
        key = jax.random.key(seed)
        ks = jax.random.split(key, 7)
        x = jax.random.normal(ks[0], (B, S, D), jnp.float32)
        ray_mask = jax.random.bernoulli(ks[1], 0.15, (B, S, S))
        attack_mask = jax.random.bernoulli(ks[2], 0.1, (B, S, S))
        s = 1.0 / np.sqrt(D)

        def lin(k):
            k1, k2 = jax.random.split(k)
            W = jax.random.uniform(k1, (D, D), jnp.float32, -s, s)
            b = jax.random.uniform(k2, (D,), jnp.float32, -s, s)
            return (W, b)
        Wq, bq = lin(ks[3])
        Wk, bk = lin(ks[4])
        Wv, bv = lin(ks[5])
        Wo, bo = lin(ks[6])
        return dict(x=x, ray_mask=ray_mask, attack_mask=attack_mask, Wq=Wq, bq=bq, Wk=Wk, bk=bk, Wv=Wv, bv=bv, Wo=Wo, bo=bo)
    _L0_gnn_all = _L0_gnn_setup()
    _L0_gnn_in = {k: v for k, v in _L0_gnn_all.items() if k in ('Wq', 'bq', 'Wk', 'bk', 'Wv', 'bv', 'Wo', 'bo')}
    del _L0_gnn_all

    def _L1_gnn_setup():
        import jax, jax.numpy as jnp
        import numpy as np
        B, N, IN, OUT, H = (16, 512, 256, 256, 4)
        key = jax.random.key(seed)
        ks = jax.random.split(key, 10)
        s = 0.03
        return {'h': jax.random.normal(ks[0], (B, N, IN), jnp.float32), 'adj': jax.random.randint(ks[1], (B, N, N), 0, 2) > 0, 'W': jax.random.normal(ks[2], (H, OUT, IN), jnp.float32) * s, 'bW': jax.random.normal(ks[3], (H, OUT), jnp.float32) * s, 'attn': jax.random.normal(ks[4], (H, OUT, OUT), jnp.float32) * s, 'A_w': jax.random.normal(ks[5], (OUT, OUT * H), jnp.float32) * s, 'fc_w': jax.random.normal(ks[6], (OUT, IN), jnp.float32) * s, 'g1_w': jax.random.normal(ks[7], (OUT, OUT), jnp.float32) * s, 'g2_w': jax.random.normal(ks[8], (OUT, OUT), jnp.float32) * s, 'gbias': jax.random.normal(ks[9], (OUT,), jnp.float32) * s}
    _L1_gnn_all = _L1_gnn_setup()
    _L1_gnn_in = {k: v for k, v in _L1_gnn_all.items() if k in ('W', 'bW', 'attn', 'A_w', 'fc_w', 'g1_w', 'g2_w', 'gbias')}
    del _L1_gnn_all
    return {'x': x, 'adj': adj, 'L0_gnn_Wq': _L0_gnn_in['Wq'], 'L0_gnn_bq': _L0_gnn_in['bq'], 'L0_gnn_Wk': _L0_gnn_in['Wk'], 'L0_gnn_bk': _L0_gnn_in['bk'], 'L0_gnn_Wv': _L0_gnn_in['Wv'], 'L0_gnn_bv': _L0_gnn_in['bv'], 'L0_gnn_Wo': _L0_gnn_in['Wo'], 'L0_gnn_bo': _L0_gnn_in['bo'], 'L1_gnn_W': _L1_gnn_in['W'], 'L1_gnn_bW': _L1_gnn_in['bW'], 'L1_gnn_attn': _L1_gnn_in['attn'], 'L1_gnn_A_w': _L1_gnn_in['A_w'], 'L1_gnn_fc_w': _L1_gnn_in['fc_w'], 'L1_gnn_g1_w': _L1_gnn_in['g1_w'], 'L1_gnn_g2_w': _L1_gnn_in['g2_w'], 'L1_gnn_gbias': _L1_gnn_in['gbias']}

def reference(x, adj, L0_gnn_Wq, L0_gnn_bq, L0_gnn_Wk, L0_gnn_bk, L0_gnn_Wv, L0_gnn_bv, L0_gnn_Wo, L0_gnn_bo, L1_gnn_W, L1_gnn_bW, L1_gnn_attn, L1_gnn_A_w, L1_gnn_fc_w, L1_gnn_g1_w, L1_gnn_g2_w, L1_gnn_gbias):
    import jax
    import jax.numpy as jnp

    def _L0_gnn_ref(x, ray_mask, attack_mask, Wq, bq, Wk, bk, Wv, bv, Wo, bo):
        import jax, jax.numpy as jnp
        import numpy as np
        B, S, D, H = (1024, 64, 256, 8)
        HD = D // H
        SCALE = float(1.0 / np.sqrt(HD))

        def _static_masks():
            sq = np.arange(64)
            r = sq // 8
            f = sq % 8
            ri, rj = (r[:, None], r[None, :])
            fi, fj = (f[:, None], f[None, :])
            dr = np.abs(ri - rj)
            df = np.abs(fi - fj)
            eye = np.eye(64, dtype=bool)
            file_m = fi == fj
            rank_m = ri == rj
            diag_m = ri - fi == rj - fj
            adiag_m = ri + fi == rj + fj
            knight_m = (dr == 2) & (df == 1) | (dr == 1) & (df == 2) | eye
            king_m = (dr <= 1) & (df <= 1)
            return np.stack([file_m, rank_m, diag_m, adiag_m, knight_m, king_m])
        STATIC = jnp.asarray(_static_masks())
        EYE = jnp.eye(S, dtype=bool)
        Bn = x.shape[0]

        def split_heads(t):
            return t.reshape(Bn, S, H, HD).transpose(0, 2, 1, 3)
        q = split_heads(x @ Wq.T + bq)
        k = split_heads(x @ Wk.T + bk)
        v = split_heads(x @ Wv.T + bv)
        scores = jnp.einsum('bhsd,bhtd->bhst', q, k) * SCALE
        mask = jnp.concatenate([jnp.broadcast_to(STATIC[None], (Bn, 6, S, S)), (ray_mask | EYE)[:, None], (attack_mask | EYE)[:, None]], axis=1)
        scores = jnp.where(mask, scores, jnp.float32(-1000000000.0))
        attn = jax.nn.softmax(scores, axis=-1)
        out = jnp.einsum('bhst,bhtd->bhsd', attn, v)
        out = out.transpose(0, 2, 1, 3).reshape(Bn, S, D)
        return out @ Wo.T + bo

    def _L1_gnn_ref(h, adj, W, bW, attn, A_w, fc_w, g1_w, g2_w, gbias):
        import jax, jax.numpy as jnp
        import numpy as np
        B, N, IN, OUT, H = (16, 512, 256, 256, 4)
        Wh = jnp.einsum('bni,hoi->bhno', h, W) + bW[None, :, None, :]
        e = jnp.einsum('bhno,hop->bhnp', Wh, attn)
        scores = jnp.einsum('bhnp,bhmp->bhnm', e, Wh)
        A_mat = jnp.tanh(jnp.where(adj[:, None, :, :], scores, 0.0))
        hp = jax.nn.relu(jnp.einsum('bhnm,bhmo->bhno', A_mat, Wh))
        cat = jnp.transpose(hp, (0, 2, 1, 3)).reshape(hp.shape[0], hp.shape[2], -1)
        ha = cat @ A_w.T
        hf = h @ fc_w.T
        coeff = jax.nn.sigmoid(hf @ g1_w.T + ha @ g2_w.T + gbias)
        return hf * coeff + ha * (1.0 - coeff)
    x = _layernorm(x + _L0_gnn_ref(x, adj, adj, L0_gnn_Wq, L0_gnn_bq, L0_gnn_Wk, L0_gnn_bk, L0_gnn_Wv, L0_gnn_bv, L0_gnn_Wo, L0_gnn_bo), axis=-1)
    x = _layernorm(x + _L1_gnn_ref(x, adj, L1_gnn_W, L1_gnn_bW, L1_gnn_attn, L1_gnn_A_w, L1_gnn_fc_w, L1_gnn_g1_w, L1_gnn_g2_w, L1_gnn_gbias), axis=-1)
    return x

_drawn_inputs = setup_inputs


def setup_inputs(seed=0):
    import zlib

    import numpy as np

    out = dict(_drawn_inputs(seed))
    spreads = {}
    factors = {'L0_gnn_bq': 8.0, 'L0_gnn_bk': 8.0, 'L0_gnn_bv': 2.779, 'L1_gnn_gbias': 8.0}
    for name, (base, spread) in spreads.items():
        noise = np.random.default_rng([zlib.crc32(name.encode()), seed]).standard_normal(out[name].shape)
        drawn = base * np.exp(spread * noise) if base else spread * noise
        out[name] = jnp.asarray(drawn.astype(out[name].dtype))
    for name, factor in factors.items():
        out[name] = (out[name] * factor).astype(out[name].dtype)
    return out
```

```python
import numpy as np
import concourse.bass as bass
from concourse import mybir
from contextlib import ExitStack

F32 = mybir.dt.float32
F32R = mybir.dt.float32r
BF16 = mybir.dt.bfloat16
U8 = mybir.dt.uint8
ACT = mybir.ActivationFunctionType
ALU = mybir.AluOpType
AX = mybir.AxisListType

GRAPHS, S, D = 128, 64, 256
P = 128
HEADS, HD = 8, 32
H2 = 4
NG = 8
NP = NG // 2
TOK = NG * S
GROUPS = GRAPHS // NG
DC = D // P
JB = HEADS // 2
KC = H2 * DC
SCALE = float(1.0 / np.sqrt(HD))
NEG = 1.0e9
EPS = 1e-5
BANKS = 4

A_TILES = (["q0", "q1", "k0", "k1", "hT0", "hT1", "v0", "v1"]
           + [f"score{j}" for j in range(JB)] + [f"probT{j}" for j in range(JB)]
           + [f"attn{c}{b}" for c in range(DC) for b in range(2)] + ["y0", "y1"])
B_TILES = (["s"] + [f"T{n}" for n in range(KC)]
           + [f"{k}{p}" for p in range(NP) for k in ("WhL", "WhR", "gate")]
           + [f"adjscore{p}" for p in range(NP)] + [f"cat{n}" for n in range(KC)]
           + ["ha0", "ha1", "haT0", "haT1", "z0", "z1"])


def stage_kernel(nc, x, xT, adjS, adjT, masks, eye, wq, bq, wk, bk, wv, bv, wo, bo,
                 Wn, WT, bWrow, attn, AwT, fcn, fcT, g1T, g2T, gb, out):
    ctx = ExitStack()
    with ctx:
        def sem(name):
            return ctx.enter_context(nc.semaphore(name))

        place = [0]

        def at(name, shape, dt, offset):
            return nc.alloc_sbuf_tensor_at(name, shape, dt, offset=offset)

        def size(shape, dt):
            n = 4 if dt in (F32, F32R) else 2 if dt == BF16 else 1
            for s in shape[1:]:
                n *= s
            return (n + 31) // 32 * 32

        base = (nc.sbuf_base + 31) // 32 * 32

        def region(nbytes):
            off = base + place[0]
            place[0] += (nbytes + 31) // 32 * 32
            return off

        def sb(name, shape, dt=F32):
            return at(name, shape, dt, region(size(shape, dt)))

        def pair(name, shape):
            return sb(name + "_hi", shape, F32R), sb(name + "_lo", shape, F32R)

        Wq, Wk, Wv, Wo = (pair(n, [P, DC, D]) for n in ("wq", "wk", "wv", "wo"))
        Wt = pair("wt", [P, DC, H2 * D])
        G = pair("g", [P, DC, H2 * D])
        FF = pair("ff", [P, DC, 2 * D])
        Aw = pair("aw", [P, KC, D])
        G2 = pair("g2", [P, DC, D])
        U = pair("u", [P, DC, P])
        bias_q, bias_k, bias_v = (sb(n, [P, DC]) for n in ("bias_q", "bias_k", "bias_v"))
        r_bias = sb("r_bias", [P, KC])
        s0 = sb("s0", [P, 1])
        bW_all = sb("bW_all", [P, H2 * D])
        bo_all = sb("bo_all", [P, D])
        gb_all = sb("gb_all", [P, 2 * D])
        ident = sb("ident", [P, P])
        identb = sb("identb", [P, P], BF16)
        mask_static = sb("mask_static", [P, JB - 1, S], BF16)
        eye2 = sb("eye2", [P, S])
        half = sb("half", [P, NP])

        r_x, r_qk, r_S, r_PT = region(8192), region(8192), region(8192), region(8192)
        r_T, r_Wh, r_gate, r_s = region(32768), region(16384), region(8192), region(8192)
        x_hi = at("x_hi", [P, DC, TOK], F32R, r_x)
        x_lo = at("x_lo", [P, DC, TOK], F32R, r_x + 4096)
        qT = at("qT", [P, DC, TOK], F32, r_qk)
        kT = at("kT", [P, DC, TOK], F32, r_qk + 4096)
        Abuf = at("Abuf", [P, NP, H2, P], F32, r_qk)
        probs = at("probs", [P, JB, TOK], F32, r_S)
        at_hi = at("at_hi", [P, DC, TOK], F32R, r_S)
        at_lo = at("at_lo", [P, DC, TOK], F32R, r_S + 4096)
        haT_hi = at("haT_hi", [P, DC, TOK], F32R, r_S)
        haT_lo = at("haT_lo", [P, DC, TOK], F32R, r_S + 4096)
        PT = at("PT", [P, JB, NP, P], F32, r_PT)
        x_raw = at("x_raw", [P, DC, TOK], F32, r_PT)
        s_row = at("s_row", [P, TOK], F32, r_PT + 4096)
        T_hi = at("T_hi", [P, DC, H2, TOK], F32R, r_T)
        T_lo = at("T_lo", [P, DC, H2, TOK], F32R, r_T + 16384)
        cat_hi = at("cat_hi", [P, KC, TOK], F32R, r_T)
        cat_lo = at("cat_lo", [P, KC, TOK], F32R, r_T + 16384)
        Wh = at("Wh", [P, NP, H2 * D], F32, r_Wh)
        gate = at("gate", [P, NP, 2 * D], F32, r_gate)
        s_all = at("s_all", [P, H2, TOK], F32, r_s)
        ha = at("ha", [P, NP, D], F32, r_s)
        res = at("res", [P, NP, D], F32, r_s + 4096)
        v = sb("v", [P, NP, D])
        y = sb("y", [P, NP, D])
        h = sb("h", [P, NP, D])
        hT_hi, hT_lo = pair("hT", [P, DC, TOK])
        adjS_u8 = sb("adjS_u8", [P, NG, S], U8)
        adj_or = sb("adj_or", [P, NG, S], BF16)
        mask_dyn = adj_or
        adjT_u8 = sb("adjT_u8", [P, NP, P], U8)
        adjT_bf = sb("adjT_bf", [P, NP, P], BF16)
        mx = sb("mx", [P, JB, NG])
        den = sb("den", [P, JB, NG])
        stats1 = sb("stats1", [P, NP, 6])
        mv1 = sb("mv1", [P, NP, 2])
        rstd1 = sb("rstd1", [P, NP])
        stats2 = sb("stats2", [P, NP, 6])
        mv2 = sb("mv2", [P, NP, 2])
        rstd2 = sb("rstd2", [P, NP])
        W_nat = at("W_nat", [P, DC, H2, D + 1], F32, r_T)
        attn_nat = at("attn_nat", [P, DC, H2, D], F32, r_T + 8256)
        M1 = at("M1", [P, DC, H2, D + 1], F32, r_T + 16448)
        fc_nat = at("fc_nat", [P, DC, D], F32, r_T + 24704)
        g1_raw = at("g1_raw", [P, DC, D], F32, r_T + 26752)
        b_diag = at("b_diag", [P, DC, H2, P], F32, r_s)
        u_cols = at("u_cols", [P, DC, P], F32, r_PT + 4096)
        raw_q, raw_k, raw_v, raw_o = (at(n, [P, DC, D], F32, r_S + 2048 * i)
                                      for i, n in enumerate(("raw_q", "raw_k", "raw_v", "raw_o")))
        raw_W = at("raw_W", [P, DC, H2 * D], F32, r_Wh)
        raw_A = at("raw_A", [P, KC, D], F32, r_Wh + 8192)
        raw_fc = at("raw_fc", [P, DC, D], F32, r_gate)
        raw_g2 = at("raw_g2", [P, DC, D], F32, r_gate + 2048)
        raw_m = at("raw_m", [P, JB - 1, S], F32, r_gate + 4096)
        assert base + place[0] <= nc.sbuf_usable_end, (base, place[0], nc.sbuf_usable_end)

        bankA = [ctx.enter_context(nc.psum_tensor(f"bankA{b}", [P, 512], F32)) for b in range(BANKS)]
        bankB = [ctx.enter_context(nc.psum_tensor(f"bankB{b}", [P, 512], F32)) for b in range(BANKS)]

        fullA, takenA, fullB, takenB = ([sem(f"{n}{b}") for b in range(BANKS)]
                                        for n in ("fullA", "takenA", "fullB", "takenB"))
        early_in, nat_in, late_in, const_in = (sem(n) for n in ("early_in", "nat_in", "late_in", "const_in"))
        xT_in, x_in, adjS_in, adjT_in, stored = (sem(n) for n in ("xT_in", "x_in", "adjS_in", "adjT_in", "stored"))
        early_hi, late_hi, weights_ready, zeroed, prod_full, prod_read, b_placed, consts_ready = (
            sem(n) for n in ("early_hi", "late_hi", "weights_ready", "zeroed", "prod_full", "prod_read",
                             "b_placed", "consts_ready"))
        hi_placed, U_placed, U_hi = (sem(n) for n in ("hi_placed", "U_placed", "U_hi"))
        x_hi_ready, x_ready, or_ready, mask_ready, xb_ready = (
            sem(n) for n in ("x_hi_ready", "x_ready", "or_ready", "mask_ready", "xb_ready"))
        max_ready, exp_ready, sum_ready, den_ready, probs_ready = (
            sem(n) for n in ("max_ready", "exp_ready", "sum_ready", "den_ready", "probs_ready"))
        at_hi_ready, stats1_ready, mv1_ready, var1_ready, rstd1_ready, h_ready, hT_hi_ready = (
            sem(n) for n in ("at_hi_ready", "stats1_ready", "mv1_ready", "var1_ready", "rstd1_ready",
                             "h_ready", "hT_hi_ready"))
        edges_ready = sem("edges_ready")
        s_ready, T_hi_ready, tanh_ready, A_ready, cat_hi_ready, haT_hi_ready, g_ready, gate_tanh = (
            sem(n) for n in ("s_ready", "T_hi_ready", "tanh_ready", "A_ready", "cat_hi_ready",
                             "haT_hi_ready", "g_ready", "gate_tanh"))
        e_ready, res_ready, stats2_ready, mv2_ready, var2_ready, rstd2_ready, out_ready = (
            sem(n) for n in ("e_ready", "res_ready", "stats2_ready", "mv2_ready", "var2_ready",
                             "rstd2_ready", "out_ready"))

        def spot(tiles, name):
            n = tiles.index(name)
            return n % BANKS, n // BANKS, len(tiles[n % BANKS::BANKS])

        def before(which, name, g):
            b, u, n = spot(TILES[which], name)
            if name in ("hT0", "hT1"):
                if isinstance(g, int) and g == GROUPS - 1:
                    return b, n * GROUPS
                g = g + 1
            return b, g * n + u

        TILES = {"A": A_TILES, "B": B_TILES}
        BANK = {"A": bankA, "B": bankB}
        FULL = {"A": fullA, "B": fullB}
        TAKEN = {"A": takenA, "B": takenB}

        def bank_of(which, name):
            return BANK[which][spot(TILES[which], name)[0]]

        def claim(pe, which, name, g):
            b, count = before(which, name, g)
            if not isinstance(count, int) or count > 0:
                pe.wait_ge(TAKEN[which][b], count)
            return BANK[which][b]

        def filled(ins, which, name):
            ins.then_inc(FULL[which][spot(TILES[which], name)[0]], 1)

        def await_tile(eng, which, name, g):
            b, count = before(which, name, g)
            eng.wait_ge(FULL[which][b], count + 1)
            return BANK[which][b]

        def take(ins, which, name):
            ins.then_inc(TAKEN[which][spot(TILES[which], name)[0]], 1)

        def await_taken(eng, which, name, g):
            b, count = before(which, name, g)
            eng.wait_ge(TAKEN[which][b], count + 1)

        def steps(A, B, more, run):
            for stage, step in (("B", "T"), ("AB", "softmax"), ("A", "score"), ("B", "Wh"), ("A", "probT"),
                                ("B", "adjscore"), ("A", "attn"), ("B", "cat"), ("N", "x"), ("A", "y"),
                                ("B", "ha"), ("N", "qk"), ("A", "hT"), ("B", "haT"), ("N", "v"),
                                ("B", "z")):
                if (stage, step) not in run:
                    continue
                if stage == "AB":
                    run[stage, step](A, B)
                    continue
                g = A if stage == "A" else B if stage == "B" else (A + 1 if more else None)
                if g is not None:
                    run[stage, step](g)

        def whole(eng, run):
            for first in (("N", "x"), ("N", "qk"), ("setup", "g1 fc"), ("N", "v")):
                if first in run:
                    run[first](0)
            steps(0, None, True, run)
            steps(1, 0, True, run)
            with eng.Fori(2, GROUPS - 1) as i:
                steps(i, i - 1, True, run)
            steps(GROUPS - 1, GROUPS - 2, False, run)
            steps(None, GROUPS - 1, False, run)

        CONSTS = 10

        passed = sem("passed")

        def carried(eng):
            eng.sem_inc(passed, 1)

        def of_graph(t, c, b):
            return t[:, c, :].rearrange("p (q b s) -> p q b s", q=NP, b=2)[:, :, b, :]

        block = ctx.enter_context(nc.Block())

        @block.sync
        def _(sp):
            def load(dst, src, s):
                sp.dma_start(dst, src).then_inc(s, 16)

            def xT_load(g):
                load(x_raw[:], xT[bass.ds(g, 1)].rearrange("o p c t -> (o p) c t"), xT_in)

            def adjS_load(g):
                for half_ in range(2):
                    load(adjS_u8[half_ * S:half_ * S + S], adjS[bass.ds(g, 1)].rearrange("o s b t -> (o s) b t"), adjS_in)

            def x_load(g):
                load(y[:], x[bass.ds(g, 1)].rearrange("o p t d -> t (o p) d"), x_in)

            load(raw_q[:], wq, early_in)
            load(raw_k[:], wk, early_in)
            load(raw_v[:], wv, early_in)
            load(raw_o[:], wo, early_in)
            xT_load(0)
            load(W_nat[:], Wn, nat_in)
            load(attn_nat[:], attn, nat_in)
            load(fc_nat[:], fcn, nat_in)
            load(g1_raw[:], g1T, nat_in)
            for dst, src in ((bias_q, bq), (bias_k, bk), (bias_v, bv), (ident, eye)):
                load(dst[:], src, const_in)
            load(raw_m[:], masks, const_in)
            for half_ in range(2):
                load(eye2[half_ * S:half_ * S + S], eye[0:S, 0:S], const_in)
            for dst, src, n in ((bW_all[:], bWrow, H2 * D), (bo_all[:], bo, D), (gb_all[:, D:2 * D], gb, D)):
                load(dst, src.to_broadcast([P, n]), const_in)
            adjS_load(0)
            x_load(0)
            load(raw_W[:], WT, late_in)
            load(raw_A[:], AwT, late_in)
            load(raw_fc[:], fcT, late_in)
            load(raw_g2[:], g2T, late_in)

            def adjT_load(g):
                if not isinstance(g, int) or g > 0:
                    sp.wait_ge(A_ready, g * NP)
                    carried(sp)
                else:
                    sp.wait_ge(zeroed, 1)
                for b in range(2):
                    load(adjT_u8[b * S:b * S + S, :, b * S:b * S + S],
                         adjT[bass.ds(g, 1), :, b].rearrange("o m p n -> (o m) p n"), adjT_in)

            def next_loads(g):
                for c in range(DC):
                    for b in range(2):
                        await_taken(sp, "A", f"attn{c}{b}", g - 1)
                carried(sp)
                xT_load(g)
                sp.wait_ge(or_ready, g)
                carried(sp)
                adjS_load(g)

            def x_next(g):
                sp.wait_ge(h_ready, g * NP)
                carried(sp)
                x_load(g)

            def store(g):
                sp.wait_ge(out_ready, g * NP + NP)
                carried(sp)
                sp.dma_start(out[bass.ds(g, 1)].rearrange("o p t d -> t (o p) d"), res[:]).then_inc(stored, 16)

            def turn(A, B, more):
                if B is not None:
                    adjT_load(B)
                if more:
                    next_loads(A + 1)
                    x_next(A + 1)
                if B is not None:
                    store(B)

            turn(0, None, True)
            turn(1, 0, True)
            with sp.Fori(2, GROUPS - 1) as i:
                turn(i, i - 1, True)
            turn(GROUPS - 1, GROUPS - 2, False)
            turn(None, GROUPS - 1, False)
            sp.wait_ge(stored, 16 * GROUPS)

        @block.tensor
        def _(pe):
            def product(out, a, b, asel, bsel, first, last):
                pe.matmul(out, asel(a[0]), bsel(b[1]), start=first, stop=False)
                pe.matmul(out, asel(a[1]), bsel(b[0]), start=False, stop=False)
                return pe.matmul(out, asel(a[0]), bsel(b[0]), start=False, stop=last)

            def dense(out, terms):
                for n, (a, b, asel, bsel) in enumerate(terms):
                    ins = product(out, a, b, asel, bsel, n == 0, n == len(terms) - 1)
                return ins

            pe.wait_ge(nat_in, 16 * 4)
            done = 0
            for hh in range(H2):
                for pc in range(DC):
                    if done >= BANKS:
                        pe.wait_ge(prod_read, done - BANKS + 1)
                    for oc in range(DC):
                        ins = pe.matmul(bankB[done % BANKS][:, 0:D + 1], attn_nat[:, oc, hh, pc * P:pc * P + P],
                                        W_nat[:, oc, hh, :], start=oc == 0, stop=oc == DC - 1)
                    ins.then_inc(prod_full, 1)
                    done += 1
            for hh in range(H2):
                for dc in range(DC):
                    pe.wait_ge(prod_read, max(done - BANKS + 1, DC * hh + DC))
                    for pc in range(DC):
                        ins = pe.matmul(bankB[done % BANKS][:, 0:D + 1], M1[:, pc, hh, dc * P:dc * P + P],
                                        W_nat[:, pc, hh, :], start=pc == 0, stop=pc == DC - 1)
                    ins.then_inc(prod_full, 1)
                    done += 1
            pe.wait_ge(prod_read, done - BANKS + 1)
            for n in range(KC):
                for pc in range(DC):
                    ins = pe.matmul(bankB[done % BANKS][:, n:n + 1], W_nat[:, pc, n // DC, (n % DC) * P:(n % DC) * P + P],
                                    M1[:, pc, n // DC, D:D + 1], start=pc == 0, stop=pc == DC - 1)
            ins.then_inc(prod_full, 1)
            done += 1
            pe.wait_ge(prod_read, done - BANKS + 1)
            pe.wait_ge(b_placed, H2)
            for n in range(H2 * DC):
                ins = pe.matmul(bankB[done % BANKS][:, 0:1], b_diag[:, n % DC, n // DC, :], M1[:, n % DC, n // DC, D:D + 1],
                                start=n == 0, stop=n == H2 * DC - 1)
            ins.then_inc(prod_full, 1)
            done += 1
            pe.wait_ge(prod_read, done)
            pe.wait_ge(weights_ready, 9)
            pe.wait_ge(consts_ready, 2)

            end = filled

            def qk(g):
                pe.wait_ge(x_ready, g + 1)
                for n, w in (("q", Wq), ("k", Wk)):
                    for c in range(DC):
                        claim(pe, "A", f"{n}{c}", g)
                        end(dense(bank_of("A", f"{n}{c}")[:], [
                            (w, (x_hi, x_lo), lambda t, k=k: t[:, k, c * P:c * P + P], lambda t, k=k: t[:, k, :])
                            for k in range(DC)]), "A", f"{n}{c}")

            def values(g):
                for t2 in range(2):
                    claim(pe, "A", f"v{t2}", g)
                    for q in range(2):
                        p = 2 * t2 + q
                        ins = dense(bank_of("A", f"v{t2}")[:, q * D:q * D + D], [
                            ((x_hi, x_lo), Wv, lambda t, k=k: t[:, k, p * P:p * P + P], lambda t, k=k: t[:, k, :])
                            for k in range(DC)])
                    end(ins, "A", f"v{t2}")

            def scores(g):
                pe.wait_ge(mask_ready, g + 1)
                for j in range(JB):
                    claim(pe, "A", f"score{j}", g)
                    m = mask_dyn[:] if j == JB - 1 else mask_static[:, j:j + 1, :].to_broadcast([P, NG, S])
                    pe.matmul(bank_of("A", f"score{j}")[:].rearrange("p (b t) -> p b t", b=NG), identb[:], m,
                              start=True, stop=False, skip_group_check=True)
                for n in ("q0", "q1", "k0", "k1"):
                    await_taken(pe, "A", n, g)
                for b in range(NG):
                    for c in range(DC):
                        for j in range(JB):
                            rows = slice(HD * j, HD * j + HD)
                            ins = pe.matmul(bank_of("A", f"score{j}")[c * S:c * S + S, b * S:b * S + S],
                                            qT[rows, c, b * S:b * S + S], kT[rows, c, b * S:b * S + S],
                                            start=False, stop=True, skip_group_check=True)
                            if b == NG - 1 and c == DC - 1:
                                end(ins, "A", f"score{j}")

            def probs_T(g):
                for j in range(JB):
                    pe.wait_ge(probs_ready, g * JB + (j + 1))
                    claim(pe, "A", f"probT{j}", g)
                    for p in range(NP):
                        ins = pe.transpose(bank_of("A", f"probT{j}")[:, p * P:p * P + P], probs[:, j, p * P:p * P + P], ident[:])
                    end(ins, "A", f"probT{j}")

            def attention(g):
                for j in range(JB):
                    await_taken(pe, "A", f"probT{j}", g)
                for t2 in range(2):
                    await_taken(pe, "A", f"v{t2}", g)
                for c in range(DC):
                    for b in range(2):
                        claim(pe, "A", f"attn{c}{b}", g)
                    carried(pe)
                    for p in range(NP):
                        for j in range(JB):
                            for b in range(2):
                                ins = pe.matmul(bank_of("A", f"attn{c}{b}")[HD * j:HD * j + HD, p * S:p * S + S],
                                                v[b * S:b * S + S, p, c * P + HD * j:c * P + HD * j + HD],
                                                PT[b * S:b * S + S, j, p, c * S:c * S + S], start=True, stop=True)
                                if p == NP - 1 and j == JB - 1:
                                    end(ins, "A", f"attn{c}{b}")

            def project(g):
                for c in range(DC):
                    for b in range(2):
                        await_taken(pe, "A", f"attn{c}{b}", g)
                for t2 in range(2):
                    claim(pe, "A", f"y{t2}", g)
                    for q in range(2):
                        p = 2 * t2 + q
                        ins = dense(bank_of("A", f"y{t2}")[:, q * D:q * D + D], [
                            ((at_hi, at_lo), Wo, lambda t, k=k: t[:, k, p * P:p * P + P], lambda t, k=k: t[:, k, :])
                            for k in range(DC)])
                    end(ins, "A", f"y{t2}")

            def transposed(src, which, names):
                for c in range(DC):
                    claim(pe, which, names[c], names[2])
                    for p in range(NP):
                        ins = pe.transpose(bank_of(which, names[c])[:, p * P:p * P + P], src[:, p, c * P:c * P + P], ident[:])
                    end(ins, which, names[c])

            def gate_weights(g):
                for c in range(DC):
                    bank = claim(pe, "A", f"hT{c}", -1)
                    for oc in range(DC):
                        ins = pe.matmul(bank[:, 0:D], fc_nat[:, oc, c * P:c * P + P], g1_raw[:, oc, :],
                                        start=oc == 0, stop=oc == DC - 1)
                    filled(ins, "A", f"hT{c}")

            def h_T(g):
                pe.wait_ge(h_ready, g * NP + NP)
                transposed(h, "A", ("hT0", "hT1", g))

            def T_and_s(g):
                for c in range(DC):
                    await_taken(pe, "A", f"hT{c}", g)
                claim(pe, "B", "s", g)
                end(dense(bank_of("B", "s")[:], [
                    (U, (hT_hi, hT_lo), lambda t, k=k: t[:, k, :], lambda t, k=k: t[:, k, :])
                    for k in range(DC)]), "B", "s")
                for n in range(KC):
                    claim(pe, "B", f"T{n}", g)
                    end(dense(bank_of("B", f"T{n}")[:], [
                        (G, (hT_hi, hT_lo), lambda t, k=k: t[:, k, n * P:n * P + P], lambda t, k=k: t[:, k, :])
                        for k in range(DC)]), "B", f"T{n}")

            def W_h(g):
                for p in range(NP):
                    for name, w, off in (("WhL", Wt, 0), ("WhR", Wt, 2 * D), ("gate", FF, 0)):
                        claim(pe, "B", f"{name}{p}", g)
                        end(dense(bank_of("B", f"{name}{p}")[:], [
                            ((hT_hi, hT_lo), w, lambda t, k=k: t[:, k, p * P:p * P + P],
                             lambda t, k=k: t[:, k, off:off + 2 * D]) for k in range(DC)]), "B", f"{name}{p}")

            def adj_scores(g):
                for n in range(KC - BANKS, KC):
                    await_taken(pe, "B", f"T{n}", g)
                for p in range(NP):
                    claim(pe, "B", f"adjscore{p}", g)
                    end(dense(bank_of("B", f"adjscore{p}")[:].rearrange("p (h n) -> p h n", h=H2), [
                        ((hT_hi, hT_lo), (T_hi, T_lo), lambda t, k=k: t[:, k, p * P:p * P + P],
                         lambda t, k=k: t[:, k, :, p * P:p * P + P]) for k in range(DC)]), "B", f"adjscore{p}")

            def cat(g):
                for name in ("WhL2", "WhR2", "WhL3", "WhR3"):
                    await_taken(pe, "B", name, g)
                pe.wait_ge(A_ready, g * NP + NP)
                for n in range(KC):
                    claim(pe, "B", f"cat{n}", g)
                    for p in range(NP):
                        ins = pe.matmul(bank_of("B", f"cat{n}")[:, p * P:p * P + P], Wh[:, p, n * P:n * P + P],
                                        Abuf[:, p, n // DC, :], start=True, stop=True)
                    end(ins, "B", f"cat{n}")

            def h_a(g):
                for t2 in range(2):
                    claim(pe, "B", f"ha{t2}", g)
                    for q in range(2):
                        p = 2 * t2 + q
                        for k in range(KC):
                            if p == 0:
                                await_taken(pe, "B", f"cat{k}", g)
                            ins = product(bank_of("B", f"ha{t2}")[:, q * D:q * D + D], (cat_hi, cat_lo), Aw,
                                          lambda t: t[:, k, p * P:p * P + P], lambda t: t[:, k, :], k == 0, k == KC - 1)
                    end(ins, "B", f"ha{t2}")

            def ha_T(g):
                for t2 in range(2):
                    await_taken(pe, "B", f"ha{t2}", g)
                transposed(ha, "B", ("haT0", "haT1", g))

            def gate_z(g):
                for c in range(DC):
                    await_taken(pe, "B", f"haT{c}", g)
                for t2 in range(2):
                    claim(pe, "B", f"z{t2}", g)
                    for q in range(2):
                        p = 2 * t2 + q
                        ins = dense(bank_of("B", f"z{t2}")[:, q * D:q * D + D], [
                            ((haT_hi, haT_lo), G2, lambda t, k=k: t[:, k, p * P:p * P + P], lambda t, k=k: t[:, k, :])
                            for k in range(DC)])
                    end(ins, "B", f"z{t2}")

            whole(pe, {("setup", "g1 fc"): gate_weights, ("N", "qk"): qk, ("N", "v"): values, ("A", "score"): scores, ("A", "probT"): probs_T,
                       ("A", "attn"): attention, ("A", "y"): project, ("A", "hT"): h_T, ("B", "T"): T_and_s,
                       ("B", "Wh"): W_h, ("B", "adjscore"): adj_scores, ("B", "cat"): cat, ("B", "ha"): h_a,
                       ("B", "haT"): ha_T, ("B", "z"): gate_z})

        @block.scalar
        def _(act):
            act.wait_ge(early_in, 16 * 4)
            for w, raw in ((Wq, raw_q), (Wk, raw_k), (Wv, raw_v), (Wo, raw_o)):
                act.activation(w[0][:], raw[:], ACT.Copy).then_inc(early_hi, 1)
            act.wait_ge(const_in, 16 * CONSTS)
            act.activation(identb[:], ident[:], ACT.Copy).then_inc(consts_ready, 1)
            act.activation(mask_static[:], raw_m[:], ACT.Copy).then_inc(consts_ready, 1)
            act.wait_ge(late_in, 16 * 4)
            for w, raw in ((Wt[0][:], raw_W), (Aw[0][:], raw_A), (FF[0][:, :, 0:D], raw_fc), (G2[0][:], raw_g2)):
                act.activation(w, raw[:], ACT.Copy).then_inc(late_hi, 1)

            def x_split(g):
                act.wait_ge(xT_in, g * 16 + 16)
                act.activation(x_hi[:], x_raw[:], ACT.Copy).then_inc(x_hi_ready, 1)

            def qk(g):
                for n, dst, bias in (("q", qT, bias_q), ("k", kT, bias_k)):
                    for c in range(DC):
                        bank = await_tile(act, "A", f"{n}{c}", g)
                        take(act.activation(dst[:, c, :], bank[:], ACT.Identity, bias=bias[:, c:c + 1]),
                             "A", f"{n}{c}")

            def values(g):
                for t2 in range(2):
                    bank = await_tile(act, "A", f"v{t2}", g)
                    take(act.activation(v[:, 2 * t2:2 * t2 + 2, :], bank[:].rearrange("p (q d) -> p q d", q=2),
                                        ACT.Copy), "A", f"v{t2}")

            def exps(g):
                for j in range(JB):
                    await_taken(act, "A", f"score{j}", g)
                    act.activation(probs[:, j, :], probs[:, j, :], ACT.Exp, scale=SCALE).then_inc(exp_ready, 1)

            def probs_T(g):
                for j in range(JB):
                    bank = await_tile(act, "A", f"probT{j}", g)
                    take(act.activation(PT[:, j, :, :], bank[:].rearrange("p (q s) -> p q s", q=NP), ACT.Copy),
                         "A", f"probT{j}")

            def attention(g):
                for c in range(DC):
                    for b in range(2):
                        bank = await_tile(act, "A", f"attn{c}{b}", g)
                        act.activation(of_graph(at_hi, c, b), bank[:, 0:NP * S].rearrange("p (q s) -> p q s", q=NP),
                                       ACT.Identity, bias=bias_v[:, c:c + 1]).then_inc(at_hi_ready, 1)

            def h_T(g):
                for c in range(DC):
                    bank = await_tile(act, "A", f"hT{c}", g)
                    act.activation(hT_hi[:, c, :], bank[:], ACT.Copy).then_inc(hT_hi_ready, 1)

            def T_and_s(g):
                bank = await_tile(act, "B", "s", g)
                if not isinstance(g, int) or g > 0:
                    act.wait_ge(s_ready, g * H2)
                take(act.activation(s_row[:], bank[:], ACT.Identity, bias=s0[:, 0:1]), "B", "s")
                for n in range(KC):
                    bank = await_tile(act, "B", f"T{n}", g)
                    act.activation(T_hi[:, n % DC, n // DC, :], bank[:], ACT.Identity, bias=r_bias[:, n:n + 1]) \
                       .then_inc(T_hi_ready, 1)

            def adj_scores(g):
                for p in range(NP):
                    await_taken(act, "B", f"adjscore{p}", g)
                    act.activation(Abuf[:, p, :, :], Abuf[:, p, :, :], ACT.Tanh).then_inc(tanh_ready, 1)

            def cat(g):
                for n in range(KC):
                    bank = await_tile(act, "B", f"cat{n}", g)
                    act.activation(cat_hi[:, n, :], bank[:], ACT.Relu).then_inc(cat_hi_ready, 1)

            def h_a(g):
                for t2 in range(2):
                    bank = await_tile(act, "B", f"ha{t2}", g)
                    take(act.activation(ha[:, 2 * t2:2 * t2 + 2, :], bank[:].rearrange("p (q d) -> p q d", q=2),
                                        ACT.Copy), "B", f"ha{t2}")

            def ha_T(g):
                for c in range(DC):
                    bank = await_tile(act, "B", f"haT{c}", g)
                    act.activation(haT_hi[:, c, :], bank[:], ACT.Copy).then_inc(haT_hi_ready, 1)

            def gate_z(g):
                for t2 in range(2):
                    await_taken(act, "B", f"z{t2}", g)
                    part = gate[:, 2 * t2:2 * t2 + 2, D:2 * D]
                    act.activation(part, part, ACT.Tanh, scale=0.5).then_inc(gate_tanh, 1)

            whole(act, {("N", "x"): x_split, ("N", "qk"): qk, ("N", "v"): values, ("A", "score"): exps,
                        ("A", "probT"): probs_T, ("A", "attn"): attention, ("A", "hT"): h_T,
                        ("B", "T"): T_and_s, ("B", "adjscore"): adj_scores, ("B", "cat"): cat,
                        ("B", "ha"): h_a, ("B", "haT"): ha_T, ("B", "z"): gate_z})

        @block.vector
        def _(dve):
            dve.memset(b_diag[:], 0.0).then_inc(zeroed, 1)
            dve.memset(u_cols[:], 0.0).then_inc(zeroed, 1)
            dve.memset(gb_all[:, 0:D], 0.0).then_inc(zeroed, 1)
            dve.wait_ge(zeroed, 4)
            dve.wait_ge(nat_in, 16 * 4)
            for hh in range(H2):
                dve.tensor_copy(b_diag[:, :, hh, 32 * hh:32 * hh + 1], W_nat[:, :, hh, D:D + 1]).then_inc(b_placed, 1)
            done = 0

            def product_out():
                dve.wait_ge(prod_full, done + 1)
                return bankB[done % BANKS]

            for n in range(H2 * DC):
                dve.tensor_copy(M1[:, n % DC, n // DC, :], product_out()[:, 0:D + 1]).then_inc(prod_read, 1)
                done += 1
            for n in range(H2 * DC):
                hh, dc = n // DC, n % DC
                bank = product_out()
                part = slice(hh * D, hh * D + D)
                dve.tensor_copy(u_cols[:, dc, 32 * hh:32 * hh + 1], bank[:, D:D + 1]).then_inc(U_placed, 1)
                dve.tensor_copy(G[0][:, dc, part], bank[:, 0:D]).then_inc(hi_placed, 1)
                dve.wait_ge(hi_placed, n + 1)
                dve.tensor_tensor(G[1][:, dc, part], bank[:, 0:D], G[0][:, dc, part].bitcast(F32), ALU.subtract) \
                   .then_inc(prod_read, 1)
                done += 1
            dve.tensor_copy(r_bias[:], product_out()[:, 0:KC]).then_inc(prod_read, 1)
            done += 1
            dve.tensor_copy(s0[:], product_out()[:, 0:1]).then_inc(prod_read, 1)
            done += 1
            dve.wait_ge(U_placed, H2 * DC)
            dve.tensor_copy(U[0][:], u_cols[:]).then_inc(U_hi, 1)
            dve.wait_ge(U_hi, 1)
            dve.tensor_tensor(U[1][:], u_cols[:], U[0][:].bitcast(F32), ALU.subtract).then_inc(weights_ready, 1)
            for n, (w, raw) in enumerate(((Wq, raw_q), (Wk, raw_k), (Wv, raw_v), (Wo, raw_o))):
                dve.wait_ge(early_hi, n + 1)
                dve.tensor_tensor(w[1][:], raw[:], w[0][:].bitcast(F32), ALU.subtract).then_inc(weights_ready, 1)
            for n, (w, raw) in enumerate(((Wt, raw_W), (Aw, raw_A), (FF, raw_fc), (G2, raw_g2))):
                dve.wait_ge(late_hi, n + 1)
                hi, lo = (t[:, :, 0:D] if w is FF else t[:] for t in w)
                dve.tensor_tensor(lo, raw[:], hi.bitcast(F32), ALU.subtract).then_inc(weights_ready, 1)
            dve.wait_ge(const_in, 16 * CONSTS)

            def low(out, bank, hi, which, name, bias=0.0, op=ALU.add):
                take(dve.scalar_tensor_tensor(out=out, in0=bank, scalar=bias, in1=hi.bitcast(F32), op0=op,
                                              op1=ALU.subtract), which, name)

            def gate_weights(g):
                for c in range(DC):
                    bank = await_tile(dve, "A", f"hT{c}", -1)
                    hi, lo = (t[:, c, D:2 * D] for t in FF)
                    dve.tensor_copy(hi, bank[:, 0:D]).then_inc(hi_placed, 1)
                    dve.wait_ge(hi_placed, H2 * DC + c + 1)
                    low(lo, bank[:, 0:D], hi, "A", f"hT{c}")

            def mask(g):
                dve.wait_ge(adjS_in, g * 32 + 32)
                dve.tensor_tensor(adj_or[:], adjS_u8[:], eye2[:, 0:S].unsqueeze(1).to_broadcast([P, NG, S]),
                                  ALU.max).then_inc(or_ready, 1)

            def T_low(g):
                for n in range(KC):
                    dve.wait_ge(T_hi_ready, g * KC + (n + 1))
                    low(T_lo[:, n % DC, n // DC, :], bank_of("B", f"T{n}")[:], T_hi[:, n % DC, n // DC, :], "B",
                        f"T{n}", r_bias[:, n:n + 1])

            def softmax_and_Wh(A, B):
                def shift(j):
                    bank = await_tile(dve, "A", f"score{j}", A)
                    view = bank[:].rearrange("p (b t) -> p b t", b=NG)
                    dve.tensor_reduce(mx[:, j, :], view, AX.X, ALU.max).then_inc(max_ready, 1)
                    dve.wait_ge(max_ready, A * JB + (j + 1))
                    take(dve.tensor_tensor(probs[:, j, :].rearrange("p (b t) -> p b t", b=NG), view,
                                           mx[:, j, :].unsqueeze(2).to_broadcast([P, NG, S]), ALU.subtract),
                         "A", f"score{j}")

                def total(j):
                    dve.wait_ge(exp_ready, A * JB + (j + 1))
                    dve.tensor_reduce(den[:, j, :], probs[:, j, :].rearrange("p (b t) -> p b t", b=NG), AX.X,
                                      ALU.add).then_inc(sum_ready, 1)
                    dve.wait_ge(sum_ready, A * JB + (j + 1))
                    dve.reciprocal(den[:, j, :], den[:, j, :]).then_inc(den_ready, 1)

                def Wh_out(p):
                    for name, dst, bias in (("WhL", Wh[:, p, 0:2 * D], bW_all[:, 0:2 * D]),
                                            ("WhR", Wh[:, p, 2 * D:4 * D], bW_all[:, 2 * D:4 * D]),
                                            ("gate", gate[:, p, :], gb_all[:])):
                        bank = await_tile(dve, "B", f"{name}{p}", B)
                        take(dve.tensor_tensor(dst, bank[:], bias, ALU.add), "B", f"{name}{p}")

                for f, n in ((shift, 0), (shift, 1), (Wh_out, 0), (shift, 2), (total, 0), (shift, 3), (total, 1),
                             (Wh_out, 1), (total, 2), (total, 3), (Wh_out, 2), (Wh_out, 3)):
                    if (B if f is Wh_out else A) is not None:
                        f(n)

            def adj_scores(g):
                dve.wait_ge(s_ready, g * H2 + H2)
                for p in range(NP):
                    bank = await_tile(dve, "B", f"adjscore{p}", g)
                    take(dve.tensor_tensor(Abuf[:, p, :, :], bank[:].rearrange("p (h n) -> p h n", h=H2),
                                           s_all[:, :, p * P:p * P + P], ALU.add), "B", f"adjscore{p}")

            def attention(g):
                for c in range(DC):
                    for b in range(2):
                        dve.wait_ge(at_hi_ready, g * 4 + (2 * c + b + 1))
                        bank = bank_of("A", f"attn{c}{b}")[:, 0:NP * S].rearrange("p (q s) -> p q s", q=NP)
                        low(of_graph(at_lo, c, b), bank, of_graph(at_hi, c, b), "A", f"attn{c}{b}", bias_v[:, c:c + 1])

            def cat_low(g):
                for n in range(KC):
                    dve.wait_ge(cat_hi_ready, g * KC + (n + 1))
                    low(cat_lo[:, n, :], bank_of("B", f"cat{n}")[:], cat_hi[:, n, :], "B", f"cat{n}", 0.0, ALU.max)

            def moments(g, src, stats, mv, stats_sem, mv_sem):
                for p in range(NP):
                    dve.bn_stats(stats[:, p, :], src[:, p, :]).then_inc(stats_sem, 1)
                dve.wait_ge(stats_sem, g * NP + NP)
                carried(dve)
                for p in range(NP):
                    dve.bn_aggr(mv[:, p, :], stats[:, p, :]).then_inc(mv_sem, 1)

            def residual(g):
                dve.wait_ge(xb_ready, g + 1)
                for t2 in range(2):
                    bank = await_tile(dve, "A", f"y{t2}", g)
                    part = y[:, 2 * t2:2 * t2 + 2, :]
                    take(dve.tensor_tensor(part, bank[:].rearrange("p (q d) -> p q d", q=2), part, ALU.add),
                         "A", f"y{t2}")
                for t2 in range(2):
                    await_taken(dve, "A", f"y{t2}", g)
                moments(g, y, stats1, mv1, stats1_ready, mv1_ready)

            def normed(g, dst, src, mv, rstd, rstd_sem, done_sem):
                dve.wait_ge(rstd_sem, g + 1)
                for p in range(NP):
                    dve.tensor_scalar(dst[:, p, :], src[:, p, :], mv[:, p, 0:1], rstd[:, p:p + 1], ALU.subtract,
                                      ALU.mult).then_inc(done_sem, 1)

            def h_a(g):
                for t2 in range(2):
                    part = slice(2 * t2, 2 * t2 + 2)
                    await_taken(dve, "B", f"ha{t2}", g)
                    dve.tensor_tensor(res[:, part, :], h[:, part, :], ha[:, part, :], ALU.add).then_inc(g_ready, 1)
                    dve.tensor_tensor(gate[:, part, 0:D], gate[:, part, 0:D], ha[:, part, :], ALU.subtract) \
                       .then_inc(g_ready, 1)

            def h_T(g):
                if not isinstance(g, int) or g > 0:
                    dve.wait_ge(g_ready, g * 4)
                normed(g, h, y, mv1, rstd1, rstd1_ready, h_ready)
                for c in range(DC):
                    dve.wait_ge(hT_hi_ready, g * DC + (c + 1))
                    low(hT_lo[:, c, :], bank_of("A", f"hT{c}")[:], hT_hi[:, c, :], "A", f"hT{c}")

            def ha_T(g):
                for c in range(DC):
                    dve.wait_ge(haT_hi_ready, g * DC + (c + 1))
                    low(haT_lo[:, c, :], bank_of("B", f"haT{c}")[:], haT_hi[:, c, :], "B", f"haT{c}")

            def gate_z(g):
                for t2 in range(2):
                    bank = await_tile(dve, "B", f"z{t2}", g)
                    part = gate[:, 2 * t2:2 * t2 + 2, D:2 * D]
                    take(dve.tensor_tensor(part, bank[:].rearrange("p (q d) -> p q d", q=2), part, ALU.add),
                         "B", f"z{t2}")
                dve.wait_ge(g_ready, g * 4 + 4)
                for t2 in range(2):
                    part = slice(2 * t2, 2 * t2 + 2)
                    dve.wait_ge(gate_tanh, g * 2 + (t2 + 1))
                    dve.scalar_tensor_tensor(out=gate[:, part, 0:D], in0=gate[:, part, D:2 * D], scalar=1.0,
                                             in1=gate[:, part, 0:D], op0=ALU.add, op1=ALU.mult).then_inc(e_ready, 1)
                for t2 in range(2):
                    part = slice(2 * t2, 2 * t2 + 2)
                    dve.wait_ge(e_ready, g * 2 + (t2 + 1))
                    dve.scalar_tensor_tensor(out=res[:, part, :], in0=gate[:, part, 0:D], scalar=0.5,
                                             in1=res[:, part, :], op0=ALU.mult, op1=ALU.add).then_inc(res_ready, 1)
                dve.wait_ge(res_ready, g * 2 + 2)
                moments(g, res, stats2, mv2, stats2_ready, mv2_ready)
                normed(g, res, res, mv2, rstd2, rstd2_ready, out_ready)

            whole(dve, {("setup", "g1 fc"): gate_weights, ("N", "x"): mask, ("B", "T"): T_low, ("AB", "softmax"): softmax_and_Wh,
                        ("B", "adjscore"): adj_scores, ("A", "attn"): attention, ("B", "cat"): cat_low,
                        ("A", "y"): residual, ("B", "ha"): h_a, ("A", "hT"): h_T, ("B", "haT"): ha_T,
                        ("B", "z"): gate_z})

        @block.gpsimd
        def _(pool):
            pool.memset(half[:], -0.5).then_inc(consts_ready, 1)
            pool.memset(adjT_u8[:], 0.0).then_inc(zeroed, 1)
            pool.wait_ge(const_in, 16 * CONSTS)

            def x_low(g):
                pool.wait_ge(x_hi_ready, g + 1)
                pool.tensor_tensor(x_lo[:], x_raw[:], x_hi[:].bitcast(F32), ALU.subtract).then_inc(x_ready, 1)
                pool.wait_ge(or_ready, g + 1)
                carried(pool)
                pool.tensor_scalar(adj_or[:], adj_or[:], NEG, -NEG, ALU.mult, ALU.add).then_inc(mask_ready, 1)

            def s_spread(g):
                await_taken(pool, "B", "s", g)
                if not isinstance(g, int) or g > 0:
                    pool.wait_ge(stored, g * 16)
                for hh in range(H2):
                    carried(pool)
                    pool.partition_broadcast(s_all[:, hh, :], s_row[32 * hh:32 * hh + 1, :]).then_inc(s_ready, 1)
                    pool.wait_ge(s_ready, g * H2 + (hh + 1))

            def probs_scaled(g):
                pool.wait_ge(x_in, g * 16 + 16)
                pool.tensor_tensor(y[:], y[:], bo_all[:, 0:D].unsqueeze(1).to_broadcast([P, NP, D]), ALU.add) \
                    .then_inc(xb_ready, 1)
                for j in range(JB):
                    pool.wait_ge(den_ready, g * JB + (j + 1))
                    view = probs[:, j, :].rearrange("p (b t) -> p b t", b=NG)
                    pool.tensor_tensor(view, view, den[:, j, :].unsqueeze(2).to_broadcast([P, NG, S]), ALU.mult) \
                        .then_inc(probs_ready, 1)

            def adj_masked(g):
                pool.wait_ge(adjT_in, g * 32 + 32)
                carried(pool)
                pool.tensor_copy(adjT_bf[:], adjT_u8[:]).then_inc(edges_ready, 1)
                pool.wait_ge(edges_ready, g + 1)
                for p in range(NP):
                    pool.wait_ge(tanh_ready, g * NP + (p + 1))
                    pool.tensor_tensor(Abuf[:, p, :, :], Abuf[:, p, :, :],
                                       adjT_bf[:, p:p + 1, :].to_broadcast([P, H2, P]), ALU.mult).then_inc(A_ready, 1)

            def root(g, mv, rstd, mv_sem, var_sem, rstd_sem):
                pool.wait_ge(mv_sem, g * NP + NP)
                carried(pool)
                pool.tensor_scalar(rstd[:], mv[:, :, 1], EPS, None, ALU.add).then_inc(var_sem, 1)
                pool.wait_ge(var_sem, g + 1)
                pool.tensor_tensor(rstd[:], rstd[:], half[:], ALU.pow).then_inc(rstd_sem, 1)

            whole(pool, {("N", "x"): x_low, ("B", "T"): s_spread, ("A", "score"): probs_scaled,
                         ("B", "adjscore"): adj_masked,
                         ("A", "y"): lambda g: root(g, mv1, rstd1, mv1_ready, var1_ready, rstd1_ready),
                         ("B", "z"): lambda g: root(g, mv2, rstd2, mv2_ready, var2_ready, rstd2_ready)})


def kernel(**inputs):
    import concourse.bacc as _bacc
    from concourse.bass_utils import run_bass_kernel_spmd as _run

    a = {k: np.asarray(t) for k, t in inputs.items()}
    x, adj = a["x"], a["adj"]

    def by_chunk(w):
        return w.reshape(-1, P, w.shape[-1]).transpose(1, 0, 2)

    def heads_first(w):
        return w.reshape(JB, 2, HD, -1).transpose(1, 0, 2, 3).reshape(D, -1)

    sq = np.arange(S)
    r, f = sq // 8, sq % 8
    dr, df = np.abs(r[:, None] - r[None]), np.abs(f[:, None] - f[None])
    diag = np.eye(S, dtype=bool)
    static = [df == 0, dr == 0, (r[:, None] - f[:, None]) == (r - f)[None], (r[:, None] + f[:, None]) == (r + f)[None],
              ((dr == 2) & (df == 1)) | ((dr == 1) & (df == 2)) | diag, (dr <= 1) & (df <= 1)]
    masks = np.where(np.stack(static), 0.0, -NEG).astype(np.float32)
    masks = masks.reshape(JB - 1, 2, S, S).transpose(1, 2, 0, 3).reshape(P, JB - 1, S)

    W, bW = a["L1_gnn_W"], a["L1_gnn_bW"]
    arrays = {
        "x": x.reshape(GROUPS, NP, P, D),
        "xT": x.reshape(GROUPS, TOK, DC, P).transpose(0, 3, 2, 1),
        "adjS": adj.reshape(GROUPS, NG, S, S).transpose(0, 2, 1, 3),
        "adjT": adj.reshape(GROUPS, NP, 2, S, S).transpose(0, 4, 2, 1, 3),
        "masks": masks,
        "eye": np.eye(P, dtype=np.float32),
        "wq": by_chunk(heads_first(a["L0_gnn_Wq"]).T), "bq": heads_first(a["L0_gnn_bq"]).reshape(DC, P).T,
        "wk": by_chunk(heads_first(a["L0_gnn_Wk"]).T), "bk": heads_first(a["L0_gnn_bk"]).reshape(DC, P).T,
        "wv": by_chunk(heads_first(a["L0_gnn_Wv"]).T), "bv": heads_first(a["L0_gnn_bv"]).reshape(DC, P).T,
        "wo": by_chunk(heads_first(a["L0_gnn_Wo"].T)), "bo": a["L0_gnn_bo"].reshape(1, D),
        "Wn": np.concatenate([W, bW[:, :, None]], axis=2).reshape(H2, DC, P, D + 1).transpose(2, 1, 0, 3),
        "WT": by_chunk(W.transpose(2, 0, 1).reshape(D, H2 * D)),
        "bWrow": bW.reshape(1, H2 * D),
        "attn": a["L1_gnn_attn"].reshape(H2, DC, P, D).transpose(2, 1, 0, 3),
        "AwT": by_chunk(a["L1_gnn_A_w"].T),
        "fcn": by_chunk(a["L1_gnn_fc_w"]),
        "fcT": by_chunk(a["L1_gnn_fc_w"].T),
        "g1T": by_chunk(a["L1_gnn_g1_w"].T),
        "g2T": by_chunk(a["L1_gnn_g2_w"].T),
        "gb": a["L1_gnn_gbias"].reshape(1, D),
    }
    nc = _bacc.Bacc("TRN2", target_bir_lowering=False, num_devices=1)
    arrays = {k: np.ascontiguousarray(t) for k, t in arrays.items()}
    args = {k: nc.dram_tensor(f"in_{k}", t.shape, mybir.dt.from_np(t.dtype), kind="ExternalInput").ap()
            for k, t in arrays.items()}
    out = nc.dram_tensor("out_0", (GROUPS, NP, P, D), F32, kind="ExternalOutput").ap()
    stage_kernel(nc, out=out, **args)
    got = _run(nc, [{f"in_{k}": t for k, t in arrays.items()}], core_ids=[0])
    return got.results[0]["out_0"].reshape(GRAPHS, S, D)
```

```python
import numpy as np
import concourse.bass as bass
from concourse import mybir
from contextlib import ExitStack

F32 = mybir.dt.float32
F32R = mybir.dt.float32r
BF16 = mybir.dt.bfloat16
U8 = mybir.dt.uint8
ACT = mybir.ActivationFunctionType
ALU = mybir.AluOpType
AX = mybir.AxisListType

GRAPHS, S, D = 128, 64, 256
P = 128
HEADS, HD = 8, 32
H2 = 4
NG = 8
NP = NG // 2
TOK = NG * S
GROUPS = GRAPHS // NG
DC = D // P
JB = HEADS // 2
KC = H2 * DC
SCALE = float(1.0 / np.sqrt(HD))
NEG = 1.0e9
EPS = 1e-5
BANKS = 4

A_TILES = (["q0", "q1", "k0", "k1", "hT0", "hT1", "v0", "v1"]
           + [f"score{j}" for j in range(JB)] + [f"probT{j}" for j in range(JB)]
           + [f"attn{c}{b}" for c in range(DC) for b in range(2)] + ["y0", "y1"])
B_TILES = (["s"] + [f"T{n}" for n in range(KC)]
           + [f"{k}{p}" for p in range(NP) for k in ("WhL", "WhR", "gate")]
           + [f"adjscore{p}" for p in range(NP)] + [f"cat{n}" for n in range(KC)]
           + ["ha0", "ha1", "haT0", "haT1", "z0", "z1"])


def stage_kernel(nc, x, xT, adjS, adjT, masks, eye, wq, bq, wk, bk, wv, bv, wo, bo,
                 Wn, WT, bWrow, attn, AwT, fcn, fcT, g1T, g2T, gb, out):
    ctx = ExitStack()
    with ctx:
        def sem(name):
            return ctx.enter_context(nc.semaphore(name))

        place = [0]

        def at(name, shape, dt, offset):
            return nc.alloc_sbuf_tensor_at(name, shape, dt, offset=offset)

        def size(shape, dt):
            n = 4 if dt in (F32, F32R) else 2 if dt == BF16 else 1
            for s in shape[1:]:
                n *= s
            return (n + 31) // 32 * 32

        base = (nc.sbuf_base + 31) // 32 * 32

        def region(nbytes):
            off = base + place[0]
            place[0] += (nbytes + 31) // 32 * 32
            return off

        def sb(name, shape, dt=F32):
            return at(name, shape, dt, region(size(shape, dt)))

        def pair(name, shape):
            return sb(name + "_hi", shape, F32R), sb(name + "_lo", shape, F32R)

        Wq, Wk, Wv, Wo = (pair(n, [P, DC, D]) for n in ("wq", "wk", "wv", "wo"))
        Wt = pair("wt", [P, DC, H2 * D])
        G = pair("g", [P, DC, H2 * D])
        FF = pair("ff", [P, DC, 2 * D])
        Aw = pair("aw", [P, KC, D])
        G2 = pair("g2", [P, DC, D])
        U = pair("u", [P, DC, P])
        bias_q, bias_k, bias_v = (sb(n, [P, DC]) for n in ("bias_q", "bias_k", "bias_v"))
        r_bias = sb("r_bias", [P, KC])
        s0 = sb("s0", [P, 1])
        bW_all = sb("bW_all", [P, H2 * D])
        bo_all = sb("bo_all", [P, D])
        gb_all = sb("gb_all", [P, D])
        ident = sb("ident", [P, P])
        identb = sb("identb", [P, P], BF16)
        mask_static = sb("mask_static", [P, JB - 1, S], BF16)
        eye2 = sb("eye2", [P, S])
        half = sb("half", [P, NP])

        r_x, r_qk, r_S, r_PT = region(8192), region(8192), region(8192), region(8192)
        r_T, r_Wh, r_gate, r_s = region(32768), region(16384), region(8192), region(8192)
        x_hi = at("x_hi", [P, DC, TOK], F32R, r_x)
        x_lo = at("x_lo", [P, DC, TOK], F32R, r_x + 4096)
        qT = at("qT", [P, DC, TOK], F32, r_qk)
        kT = at("kT", [P, DC, TOK], F32, r_qk + 4096)
        Abuf = at("Abuf", [P, NP, H2, P], F32, r_qk)
        probs = at("probs", [P, JB, TOK], F32, r_S)
        at_hi = at("at_hi", [P, DC, TOK], F32R, r_S)
        at_lo = at("at_lo", [P, DC, TOK], F32R, r_S + 4096)
        haT_hi = at("haT_hi", [P, DC, TOK], F32R, r_S)
        haT_lo = at("haT_lo", [P, DC, TOK], F32R, r_S + 4096)
        PT = at("PT", [P, JB, NP, P], F32, r_PT)
        x_raw = at("x_raw", [P, DC, TOK], F32, r_PT)
        s_row = at("s_row", [P, TOK], F32, r_PT + 4096)
        T = at("T", [P, DC, H2, TOK], F32, r_T + 16384)
        hT = at("hT", [P, DC, TOK], F32, r_T)
        edges = at("edges", [P, NP, H2, S], F32, r_T + 4096)
        cat_hi = at("cat_hi", [P, KC, TOK], F32R, r_T)
        cat_lo = at("cat_lo", [P, KC, TOK], F32R, r_T + 16384)
        Wh = at("Wh", [P, NP, H2 * D], F32, r_Wh)
        gate = at("gate", [P, NP, 2 * D], F32, r_gate)
        s_all = at("s_all", [P, H2, TOK], F32, r_s)
        ha = at("ha", [P, NP, D], F32, r_s)
        res = at("res", [P, NP, D], F32, r_s + 4096)
        v = sb("v", [P, NP, D])
        y = sb("y", [P, NP, D])
        h = sb("h", [P, NP, D])
        hT_hi, hT_lo = pair("hT", [P, DC, TOK])
        adjS_u8 = sb("adjS_u8", [P, NG, S], U8)
        adj_or = sb("adj_or", [P, NG, S], BF16)
        mask_dyn = adj_or
        adjT_u8 = sb("adjT_u8", [P, NP, S], U8)
        mx = sb("mx", [P, JB, NG])
        den = sb("den", [P, JB, NG])
        stats1 = sb("stats1", [P, NP, 6])
        mv1 = sb("mv1", [P, NP, 2])
        rstd1 = sb("rstd1", [P, NP])
        stats2 = sb("stats2", [P, NP, 6])
        mv2 = sb("mv2", [P, NP, 2])
        rstd2 = sb("rstd2", [P, NP])
        W_nat = at("W_nat", [P, DC, H2, D + 1], F32, r_T)
        attn_nat = at("attn_nat", [P, DC, H2, D], F32, r_T + 8256)
        M1 = at("M1", [P, DC, H2, D + 1], F32, r_T + 16448)
        fc_nat = at("fc_nat", [P, DC, D], F32, r_T + 24704)
        g1_raw = at("g1_raw", [P, DC, D], F32, r_T + 26752)
        b_diag = at("b_diag", [P, DC, H2, P], F32, r_s)
        u_cols = at("u_cols", [P, DC, P], F32, r_T + 28800)
        raw_q, raw_k, raw_v, raw_o = (at(n, [P, DC, D], F32, r_S + 2048 * i)
                                      for i, n in enumerate(("raw_q", "raw_k", "raw_v", "raw_o")))
        raw_W = at("raw_W", [P, DC, H2 * D], F32, r_Wh)
        raw_A = at("raw_A", [P, KC, D], F32, r_Wh + 8192)
        raw_fc = at("raw_fc", [P, DC, D], F32, r_gate)
        raw_g2 = at("raw_g2", [P, DC, D], F32, r_gate + 2048)
        raw_m = at("raw_m", [P, JB - 1, S], F32, r_gate + 4096)
        assert base + place[0] <= nc.sbuf_usable_end, (base, place[0], nc.sbuf_usable_end)

        bankA = [ctx.enter_context(nc.psum_tensor(f"bankA{b}", [P, 512], F32)) for b in range(BANKS)]
        bankB = [ctx.enter_context(nc.psum_tensor(f"bankB{b}", [P, 512], F32)) for b in range(BANKS)]

        fullA, takenA, fullB, takenB = ([sem(f"{n}{b}") for b in range(BANKS)]
                                        for n in ("fullA", "takenA", "fullB", "takenB"))
        early_in = [sem(f"early_in{n}") for n in range(4)]
        nat_in, late_in, const_in, gate_in, rows_in = (
            sem(n) for n in ("nat_in", "late_in", "const_in", "gate_in", "rows_in"))
        xT_in, x_in, adjS_in, adjT_in, stored = (sem(n) for n in ("xT_in", "x_in", "adjS_in", "adjT_in", "stored"))
        early_hi, late_hi, weights_ready, zeroed, prod_full, prod_read, b_placed, consts_ready = (
            sem(n) for n in ("early_hi", "late_hi", "weights_ready", "zeroed", "prod_full", "prod_read",
                             "b_placed", "consts_ready"))
        M1_ready, G_hi, FF_hi, U_placed, U_hi = (sem(n) for n in ("M1_ready", "G_hi", "FF_hi", "U_placed", "U_hi"))
        x_hi_ready, x_ready, or_ready, mask_ready, xb_ready = (
            sem(n) for n in ("x_hi_ready", "x_ready", "or_ready", "mask_ready", "xb_ready"))
        max_ready, exp_ready, sum_ready, den_ready, probs_ready = (
            sem(n) for n in ("max_ready", "exp_ready", "sum_ready", "den_ready", "probs_ready"))
        at_hi_ready, stats1_ready, mv1_ready, var1_ready, rstd1_ready, h_ready, hT_hi_ready = (
            sem(n) for n in ("at_hi_ready", "stats1_ready", "mv1_ready", "var1_ready", "rstd1_ready",
                             "h_ready", "hT_hi_ready"))
        A_zeroed, gate_biased = sem("A_zeroed"), sem("gate_biased")
        s_ready, hT_ready, tanh_ready, A_ready, cat_hi_ready, haT_hi_ready, g_ready, gate_tanh = (
            sem(n) for n in ("s_ready", "hT_ready", "tanh_ready", "A_ready", "cat_hi_ready",
                             "haT_hi_ready", "g_ready", "gate_tanh"))
        e_ready, res_ready, stats2_ready, mv2_ready, var2_ready, rstd2_ready, out_ready = (
            sem(n) for n in ("e_ready", "res_ready", "stats2_ready", "mv2_ready", "var2_ready",
                             "rstd2_ready", "out_ready"))

        def spot(tiles, name):
            n = tiles.index(name)
            return n % BANKS, n // BANKS, len(tiles[n % BANKS::BANKS])

        def before(which, name, g):
            b, u, n = spot(TILES[which], name)
            if name in ("hT0", "hT1"):
                if isinstance(g, int) and g == GROUPS - 1:
                    return b, n * GROUPS
                g = g + 1
            return b, g * n + u

        TILES = {"A": A_TILES, "B": B_TILES}
        BANK = {"A": bankA, "B": bankB}
        FULL = {"A": fullA, "B": fullB}
        TAKEN = {"A": takenA, "B": takenB}

        def bank_of(which, name):
            return BANK[which][spot(TILES[which], name)[0]]

        def claim(pe, which, name, g):
            b, count = before(which, name, g)
            if not isinstance(count, int) or count > 0:
                pe.wait_ge(TAKEN[which][b], count)
            return BANK[which][b]

        def filled(ins, which, name):
            ins.then_inc(FULL[which][spot(TILES[which], name)[0]], 1)

        def await_tile(eng, which, name, g):
            b, count = before(which, name, g)
            eng.wait_ge(FULL[which][b], count + 1)
            return BANK[which][b]

        def take(ins, which, name):
            ins.then_inc(TAKEN[which][spot(TILES[which], name)[0]], 1)

        def await_taken(eng, which, name, g):
            b, count = before(which, name, g)
            eng.wait_ge(TAKEN[which][b], count + 1)

        def steps(A, B, more, run):
            for stage, step in (("AB", "T and score"), ("B", "T"), ("L", "norm"), ("B", "s"), ("AB", "softmax"),
                                ("A", "score"), ("S", "M1"), ("B", "Wh"), ("A", "probT"),
                                ("B", "adjscore"), ("A", "attn"), ("S", "G"), ("B", "cat"), ("N", "x"), ("A", "y"), ("S", "r"),
                                ("B", "ha"), ("N", "qk"), ("A", "hT"), ("B", "haT"), ("N", "v"),
                                ("B", "z")):
                if (stage, step) not in run:
                    continue
                if stage == "AB":
                    run[stage, step](A, B)
                    continue
                g = {"A": A, "B": B, "N": A + 1 if more else None, "S": 0 if B is None and more else None,
                     "L": None if B is None or (isinstance(B, int) and B == 0) else B - 1}[stage]
                if g is not None:
                    run[stage, step](g)

        def whole(eng, run):
            for first in (("N", "x"), ("N", "qk"), ("setup", "g1 fc"), ("N", "v")):
                if first in run:
                    run[first](0)
            steps(0, None, True, run)
            steps(1, 0, True, run)
            with eng.Fori(2, GROUPS - 1) as i:
                steps(i, i - 1, True, run)
            steps(GROUPS - 1, GROUPS - 2, False, run)
            steps(None, GROUPS - 1, False, run)
            if ("L", "norm") in run:
                run["L", "norm"](GROUPS - 1)

        CONSTS = 7

        passed = sem("passed")

        def carried(eng):
            eng.sem_inc(passed, 1)

        def of_graph(t, c, b):
            return t[:, c, :].rearrange("p (q b s) -> p q b s", q=NP, b=2)[:, :, b, :]

        block = ctx.enter_context(nc.Block())

        @block.sync
        def _(sp):
            def load(dst, src, s):
                sp.dma_start(dst, src).then_inc(s, 16)

            def xT_load(g):
                load(x_raw[:], xT[bass.ds(g, 1)].rearrange("o p c t -> (o p) c t"), xT_in)

            def adjS_load(g):
                for half_ in range(2):
                    load(adjS_u8[half_ * S:half_ * S + S], adjS[bass.ds(g, 1)].rearrange("o s b t -> (o s) b t"), adjS_in)

            def x_load(g):
                load(y[:], x[bass.ds(g, 1)].rearrange("o p t d -> t (o p) d"), x_in)

            load(raw_q[:], wq, early_in[0])
            xT_load(0)
            load(raw_k[:], wk, early_in[1])
            for dst, src in ((bias_q, bq), (bias_k, bk), (bias_v, bv), (ident, eye)):
                load(dst[:], src, const_in)
            load(raw_m[:], masks, const_in)
            for half_ in range(2):
                load(eye2[half_ * S:half_ * S + S], eye[0:S, 0:S], const_in)
            load(fc_nat[:], fcn, gate_in)
            load(g1_raw[:], g1T, gate_in)
            load(raw_v[:], wv, early_in[2])
            adjS_load(0)
            load(raw_o[:], wo, early_in[3])
            load(W_nat[:], Wn, nat_in)
            load(attn_nat[:], attn, nat_in)
            x_load(0)
            for dst, src, n in ((bo_all, bo, D), (bW_all, bWrow, H2 * D), (gb_all, gb, D)):
                load(dst[:], src.to_broadcast([P, n]), rows_in)
            load(raw_W[:], WT, late_in)
            load(raw_A[:], AwT, late_in)
            load(raw_fc[:], fcT, late_in)
            load(raw_g2[:], g2T, late_in)

            def adjT_load(g):
                if not isinstance(g, int) or g > 0:
                    sp.wait_ge(A_ready, g * NP * 2)
                    carried(sp)
                load(adjT_u8[:], adjT[bass.ds(g, 1)].rearrange("o m p n -> (o m) p n"), adjT_in)

            def next_loads(g):
                for c in range(DC):
                    for b in range(2):
                        await_taken(sp, "A", f"attn{c}{b}", g - 1)
                carried(sp)
                xT_load(g)
                sp.wait_ge(or_ready, g)
                carried(sp)
                adjS_load(g)

            def x_next(g):
                sp.wait_ge(h_ready, g * NP)
                carried(sp)
                x_load(g)

            def store(g):
                sp.wait_ge(out_ready, g * NP + NP)
                carried(sp)
                sp.dma_start(out[bass.ds(g, 1)].rearrange("o p t d -> t (o p) d"), res[:]).then_inc(stored, 16)

            def turn(A, B, more):
                if B is not None:
                    adjT_load(B)
                    if not isinstance(B, int) or B > 0:
                        store(B - 1)
                if more:
                    next_loads(A + 1)
                    x_next(A + 1)

            turn(0, None, True)
            turn(1, 0, True)
            with sp.Fori(2, GROUPS - 1) as i:
                turn(i, i - 1, True)
            turn(GROUPS - 1, GROUPS - 2, False)
            turn(None, GROUPS - 1, False)
            store(GROUPS - 1)
            sp.wait_ge(stored, 16 * GROUPS)

        @block.tensor
        def _(pe):
            def product(out, a, b, asel, bsel, first, last):
                pe.matmul(out, asel(a[0]), bsel(b[1]), start=first, stop=False)
                pe.matmul(out, asel(a[1]), bsel(b[0]), start=False, stop=False)
                return pe.matmul(out, asel(a[0]), bsel(b[0]), start=False, stop=last)

            def dense(out, terms):
                for n, (a, b, asel, bsel) in enumerate(terms):
                    ins = product(out, a, b, asel, bsel, n == 0, n == len(terms) - 1)
                return ins

            def M1_products(g):
                pe.wait_ge(nat_in, 16 * 2)
                for n in range(H2 * DC):
                    hh, pc = n // DC, n % DC
                    if n >= BANKS:
                        pe.wait_ge(M1_ready, n - BANKS + 1)
                    for oc in range(DC):
                        ins = pe.matmul(bankB[n % BANKS][:, 0:D + 1], attn_nat[:, oc, hh, pc * P:pc * P + P],
                                        W_nat[:, oc, hh, :], start=oc == 0, stop=oc == DC - 1)
                    ins.then_inc(prod_full, 1)

            def G_products(g):
                pe.wait_ge(M1_ready, H2 * DC)
                for n in range(H2 * DC):
                    hh, dc = n // DC, n % DC
                    if n >= BANKS:
                        pe.wait_ge(prod_read, n - BANKS + 1)
                    for pc in range(DC):
                        ins = pe.matmul(bankB[n % BANKS][:, 0:D + 1], M1[:, pc, hh, dc * P:dc * P + P],
                                        W_nat[:, pc, hh, :], start=pc == 0, stop=pc == DC - 1)
                    ins.then_inc(prod_full, 1)

            def r_products(g):
                pe.wait_ge(prod_read, H2 * DC)
                for n in range(KC):
                    for pc in range(DC):
                        ins = pe.matmul(bankB[0][:, n:n + 1], W_nat[:, pc, n // DC, (n % DC) * P:(n % DC) * P + P],
                                        M1[:, pc, n // DC, D:D + 1], start=pc == 0, stop=pc == DC - 1)
                ins.then_inc(prod_full, 1)
                pe.wait_ge(b_placed, H2)
                for n in range(H2 * DC):
                    ins = pe.matmul(bankB[1][:, 0:1], b_diag[:, n % DC, n // DC, :], M1[:, n % DC, n // DC, D:D + 1],
                                    start=n == 0, stop=n == H2 * DC - 1)
                ins.then_inc(prod_full, 1)

            end = filled

            def qk(g):
                pe.wait_ge(x_ready, g + 1)
                for i, (n, w) in enumerate((("q", Wq), ("k", Wk))):
                    if isinstance(g, int) and g == 0:
                        pe.wait_ge(weights_ready, i + 1)
                    for c in range(DC):
                        claim(pe, "A", f"{n}{c}", g)
                        end(dense(bank_of("A", f"{n}{c}")[:], [
                            (w, (x_hi, x_lo), lambda t, k=k: t[:, k, c * P:c * P + P], lambda t, k=k: t[:, k, :])
                            for k in range(DC)]), "A", f"{n}{c}")

            def values(g):
                if isinstance(g, int) and g == 0:
                    pe.wait_ge(weights_ready, 3)
                for t2 in range(2):
                    claim(pe, "A", f"v{t2}", g)
                    for q in range(2):
                        p = 2 * t2 + q
                        ins = dense(bank_of("A", f"v{t2}")[:, q * D:q * D + D], [
                            ((x_hi, x_lo), Wv, lambda t, k=k: t[:, k, p * P:p * P + P], lambda t, k=k: t[:, k, :])
                            for k in range(DC)])
                    end(ins, "A", f"v{t2}")

            def scores(g, j):
                if j == 0:
                    pe.wait_ge(mask_ready, g + 1)
                    if isinstance(g, int) and g == 0:
                        pe.wait_ge(consts_ready, 3)
                    for n in ("q0", "q1", "k0", "k1"):
                        await_taken(pe, "A", n, g)
                bank = claim(pe, "A", f"score{j}", g)
                m = mask_dyn[:] if j == JB - 1 else mask_static[:, j:j + 1, :].to_broadcast([P, NG, S])
                pe.matmul(bank[:].rearrange("p (b t) -> p b t", b=NG), identb[:], m, start=True, stop=False,
                          skip_group_check=True)
                rows = slice(HD * j, HD * j + HD)
                for b in range(NG):
                    for c in range(DC):
                        ins = pe.matmul(bank[c * S:c * S + S, b * S:b * S + S],
                                        qT[rows, c, b * S:b * S + S], kT[rows, c, b * S:b * S + S],
                                        start=False, stop=True, skip_group_check=True)
                end(ins, "A", f"score{j}")

            def probs_T(g):
                for j in range(JB):
                    pe.wait_ge(probs_ready, g * JB + (j + 1))
                    claim(pe, "A", f"probT{j}", g)
                    for p in range(NP):
                        ins = pe.transpose(bank_of("A", f"probT{j}")[:, p * P:p * P + P], probs[:, j, p * P:p * P + P], ident[:])
                    end(ins, "A", f"probT{j}")

            def attention(g):
                for j in range(JB):
                    await_taken(pe, "A", f"probT{j}", g)
                for t2 in range(2):
                    await_taken(pe, "A", f"v{t2}", g)
                for c in range(DC):
                    for b in range(2):
                        claim(pe, "A", f"attn{c}{b}", g)
                    carried(pe)
                    for p in range(NP):
                        for j in range(JB):
                            for b in range(2):
                                ins = pe.matmul(bank_of("A", f"attn{c}{b}")[HD * j:HD * j + HD, p * S:p * S + S],
                                                v[b * S:b * S + S, p, c * P + HD * j:c * P + HD * j + HD],
                                                PT[b * S:b * S + S, j, p, c * S:c * S + S], start=True, stop=True)
                                if p == NP - 1 and j == JB - 1:
                                    end(ins, "A", f"attn{c}{b}")

            def project(g):
                if isinstance(g, int) and g == 0:
                    pe.wait_ge(weights_ready, 4)
                for c in range(DC):
                    for b in range(2):
                        await_taken(pe, "A", f"attn{c}{b}", g)
                for t2 in range(2):
                    claim(pe, "A", f"y{t2}", g)
                    for q in range(2):
                        p = 2 * t2 + q
                        ins = dense(bank_of("A", f"y{t2}")[:, q * D:q * D + D], [
                            ((at_hi, at_lo), Wo, lambda t, k=k: t[:, k, p * P:p * P + P], lambda t, k=k: t[:, k, :])
                            for k in range(DC)])
                    end(ins, "A", f"y{t2}")

            def transposed(src, which, names):
                for c in range(DC):
                    claim(pe, which, names[c], names[2])
                    for p in range(NP):
                        ins = pe.transpose(bank_of(which, names[c])[:, p * P:p * P + P], src[:, p, c * P:c * P + P], ident[:])
                    end(ins, which, names[c])

            def gate_weights(g):
                pe.wait_ge(gate_in, 16 * 2)
                for c in range(DC):
                    bank = claim(pe, "A", f"hT{c}", -1)
                    for oc in range(DC):
                        ins = pe.matmul(bank[:, 0:D], fc_nat[:, oc, c * P:c * P + P], g1_raw[:, oc, :],
                                        start=oc == 0, stop=oc == DC - 1)
                    filled(ins, "A", f"hT{c}")

            def h_T(g):
                pe.wait_ge(h_ready, g * NP + NP)
                transposed(h, "A", ("hT0", "hT1", g))

            SCORES_FROM = 4

            def s_rows(g):
                if isinstance(g, int) and g == 0:
                    pe.wait_ge(prod_read, H2 * DC + 2)
                    pe.wait_ge(weights_ready, 9)
                for c in range(DC):
                    await_taken(pe, "A", f"hT{c}", g)
                claim(pe, "B", "s", g)
                end(dense(bank_of("B", "s")[:], [
                    (U, (hT_hi, hT_lo), lambda t, k=k: t[:, k, :], lambda t, k=k: t[:, k, :])
                    for k in range(DC)]), "B", "s")

            def T_tile(g, n):
                claim(pe, "B", f"T{n}", g)
                end(dense(bank_of("B", f"T{n}")[:], [
                    (G, (hT_hi, hT_lo), lambda t, k=k: t[:, k, n * P:n * P + P], lambda t, k=k: t[:, k, :])
                    for k in range(DC)]), "B", f"T{n}")

            def T_and_scores(A, B):
                if B is not None:
                    s_rows(B)
                for n in range(KC):
                    if B is not None:
                        T_tile(B, n)
                    if A is not None and 0 <= n - SCORES_FROM < JB:
                        scores(A, n - SCORES_FROM)

            def W_h(g):
                for p in range(NP):
                    for name, w, off in (("WhL", Wt, 0), ("WhR", Wt, 2 * D), ("gate", FF, 0)):
                        claim(pe, "B", f"{name}{p}", g)
                        end(dense(bank_of("B", f"{name}{p}")[:], [
                            ((hT_hi, hT_lo), w, lambda t, k=k: t[:, k, p * P:p * P + P],
                             lambda t, k=k: t[:, k, off:off + 2 * D]) for k in range(DC)]), "B", f"{name}{p}")

            def adj_scores(g):
                for n in range(KC - BANKS, KC):
                    await_taken(pe, "B", f"T{n}", g)
                pe.wait_ge(hT_ready, g + 1)
                for p in range(NP):
                    bank = claim(pe, "B", f"adjscore{p}", g)
                    for k in range(DC):
                        for b in range(2):
                            graph = slice(p * P + b * S, p * P + b * S + S)
                            ins = pe.matmul(bank[b * S:b * S + S, 0:H2 * S].rearrange("p (h n) -> p h n", h=H2),
                                            hT[:, k, graph], T[:, k, :, graph], start=k == 0, stop=k == DC - 1)
                    end(ins, "B", f"adjscore{p}")

            def cat(g):
                for name in ("WhL2", "WhR2", "WhL3", "WhR3"):
                    await_taken(pe, "B", name, g)
                pe.wait_ge(A_ready, g * NP * 2 + NP * 2)
                pe.wait_ge(A_zeroed, 2 * g if isinstance(g, int) and g == GROUPS - 1 else g * 2 + 2)
                for n in range(KC):
                    claim(pe, "B", f"cat{n}", g)
                    for p in range(NP):
                        ins = pe.matmul(bank_of("B", f"cat{n}")[:, p * P:p * P + P], Wh[:, p, n * P:n * P + P],
                                        Abuf[:, p, n // DC, :], start=True, stop=True)
                    end(ins, "B", f"cat{n}")

            def h_a(g):
                for t2 in range(2):
                    claim(pe, "B", f"ha{t2}", g)
                    for q in range(2):
                        p = 2 * t2 + q
                        for k in range(KC):
                            if p == 0:
                                await_taken(pe, "B", f"cat{k}", g)
                            ins = product(bank_of("B", f"ha{t2}")[:, q * D:q * D + D], (cat_hi, cat_lo), Aw,
                                          lambda t: t[:, k, p * P:p * P + P], lambda t: t[:, k, :], k == 0, k == KC - 1)
                    end(ins, "B", f"ha{t2}")

            def ha_T(g):
                for t2 in range(2):
                    await_taken(pe, "B", f"ha{t2}", g)
                transposed(ha, "B", ("haT0", "haT1", g))

            def gate_z(g):
                for c in range(DC):
                    await_taken(pe, "B", f"haT{c}", g)
                for t2 in range(2):
                    claim(pe, "B", f"z{t2}", g)
                    for q in range(2):
                        p = 2 * t2 + q
                        ins = dense(bank_of("B", f"z{t2}")[:, q * D:q * D + D], [
                            ((haT_hi, haT_lo), G2, lambda t, k=k: t[:, k, p * P:p * P + P], lambda t, k=k: t[:, k, :])
                            for k in range(DC)])
                    end(ins, "B", f"z{t2}")

            whole(pe, {("setup", "g1 fc"): gate_weights, ("S", "M1"): M1_products, ("S", "G"): G_products,
                       ("S", "r"): r_products, ("N", "qk"): qk, ("N", "v"): values, ("AB", "T and score"): T_and_scores, ("A", "probT"): probs_T,
                       ("A", "attn"): attention, ("A", "y"): project, ("A", "hT"): h_T,
                       ("B", "Wh"): W_h, ("B", "adjscore"): adj_scores, ("B", "cat"): cat, ("B", "ha"): h_a,
                       ("B", "haT"): ha_T, ("B", "z"): gate_z})

        @block.scalar
        def _(act):
            def x_split(g):
                act.wait_ge(xT_in, g * 16 + 16)
                act.activation(x_hi[:], x_raw[:], ACT.Copy).then_inc(x_hi_ready, 1)

            for n, (w, raw) in enumerate(((Wq, raw_q), (Wk, raw_k), (Wv, raw_v), (Wo, raw_o))):
                act.wait_ge(early_in[n], 16)
                act.activation(w[0][:], raw[:], ACT.Copy).then_inc(early_hi, 1)
                if n == 0:
                    x_split(0)
                if n == 1:
                    act.wait_ge(const_in, 16 * CONSTS)
                    act.activation(identb[:], ident[:], ACT.Copy).then_inc(consts_ready, 1)
                    act.activation(mask_static[:], raw_m[:], ACT.Copy).then_inc(consts_ready, 1)

            def late(g):
                act.wait_ge(late_in, 16 * 4)
                for w, raw in ((Wt[0][:], raw_W), (Aw[0][:], raw_A), (FF[0][:, :, 0:D], raw_fc), (G2[0][:], raw_g2)):
                    act.activation(w, raw[:], ACT.Copy).then_inc(late_hi, 1)

            def qk(g):
                for n, dst, bias in (("q", qT, bias_q), ("k", kT, bias_k)):
                    for c in range(DC):
                        bank = await_tile(act, "A", f"{n}{c}", g)
                        take(act.activation(dst[:, c, :], bank[:], ACT.Identity, bias=bias[:, c:c + 1]),
                             "A", f"{n}{c}")

            def values(g):
                for t2 in range(2):
                    bank = await_tile(act, "A", f"v{t2}", g)
                    take(act.activation(v[:, 2 * t2:2 * t2 + 2, :], bank[:].rearrange("p (q d) -> p q d", q=2),
                                        ACT.Copy), "A", f"v{t2}")

            def exps(g):
                for j in range(JB):
                    await_taken(act, "A", f"score{j}", g)
                    act.activation(probs[:, j, :], probs[:, j, :], ACT.Exp, scale=SCALE).then_inc(exp_ready, 1)

            def probs_T(g):
                for j in range(JB):
                    bank = await_tile(act, "A", f"probT{j}", g)
                    take(act.activation(PT[:, j, :, :], bank[:].rearrange("p (q s) -> p q s", q=NP), ACT.Copy),
                         "A", f"probT{j}")

            def attention(g):
                for c in range(DC):
                    for b in range(2):
                        bank = await_tile(act, "A", f"attn{c}{b}", g)
                        act.activation(of_graph(at_hi, c, b), bank[:, 0:NP * S].rearrange("p (q s) -> p q s", q=NP),
                                       ACT.Identity, bias=bias_v[:, c:c + 1]).then_inc(at_hi_ready, 1)

            def h_T(g):
                for c in range(DC):
                    bank = await_tile(act, "A", f"hT{c}", g)
                    act.activation(hT_hi[:, c, :], bank[:], ACT.Copy).then_inc(hT_hi_ready, 1)

            def T_and_s(g):
                bank = await_tile(act, "B", "s", g)
                if not isinstance(g, int) or g > 0:
                    act.wait_ge(s_ready, g * H2)
                take(act.activation(s_row[:], bank[:], ACT.Identity, bias=s0[:, 0:1]), "B", "s")
                for n in range(KC):
                    bank = await_tile(act, "B", f"T{n}", g)
                    take(act.activation(T[:, n % DC, n // DC, :], bank[:], ACT.Identity, bias=r_bias[:, n:n + 1]),
                         "B", f"T{n}")

            def W_h(g):
                if not isinstance(g, int) or g > 0:
                    act.wait_ge(res_ready, g * 2)
                for p in range(NP):
                    bank = await_tile(act, "B", f"gate{p}", g)
                    take(act.activation(gate[:, p, :], bank[:], ACT.Copy), "B", f"gate{p}")

            def adj_scores(g):
                for p in range(NP):
                    await_taken(act, "B", f"adjscore{p}", g)
                    act.activation(edges[:, p, :, :], edges[:, p, :, :], ACT.Tanh).then_inc(tanh_ready, 1)

            def cat(g):
                for n in range(KC):
                    bank = await_tile(act, "B", f"cat{n}", g)
                    act.activation(cat_hi[:, n, :], bank[:], ACT.Relu).then_inc(cat_hi_ready, 1)

            def h_a(g):
                for t2 in range(2):
                    bank = await_tile(act, "B", f"ha{t2}", g)
                    take(act.activation(ha[:, 2 * t2:2 * t2 + 2, :], bank[:].rearrange("p (q d) -> p q d", q=2),
                                        ACT.Copy), "B", f"ha{t2}")

            def ha_T(g):
                for c in range(DC):
                    bank = await_tile(act, "B", f"haT{c}", g)
                    act.activation(haT_hi[:, c, :], bank[:], ACT.Copy).then_inc(haT_hi_ready, 1)

            def gate_z(g):
                for t2 in range(2):
                    await_taken(act, "B", f"z{t2}", g)
                    part = gate[:, 2 * t2:2 * t2 + 2, D:2 * D]
                    act.activation(part, part, ACT.Tanh, scale=0.5).then_inc(gate_tanh, 1)

            def M1_copies(g):
                for n in range(H2 * DC):
                    act.wait_ge(prod_full, n + 1)
                    act.activation(M1[:, n % DC, n // DC, :], bankB[n % BANKS][:, 0:D + 1], ACT.Copy) \
                       .then_inc(M1_ready, 1)

            def G_high(g):
                for n in range(H2 * DC):
                    act.wait_ge(prod_full, H2 * DC + n + 1)
                    hh, dc = n // DC, n % DC
                    act.activation(G[0][:, dc, hh * D:hh * D + D], bankB[n % BANKS][:, 0:D], ACT.Copy) \
                       .then_inc(G_hi, 1)

            def later_x_split(g):
                if not isinstance(g, int) or g > 0:
                    x_split(g)

            whole(act, {("N", "x"): later_x_split, ("S", "M1"): M1_copies, ("S", "G"): G_high,
                        ("S", "r"): late, ("N", "qk"): qk, ("N", "v"): values, ("A", "score"): exps,
                        ("A", "probT"): probs_T, ("A", "attn"): attention, ("A", "hT"): h_T,
                        ("B", "T"): T_and_s, ("B", "Wh"): W_h, ("B", "adjscore"): adj_scores, ("B", "cat"): cat,
                        ("B", "ha"): h_a, ("B", "haT"): ha_T, ("B", "z"): gate_z})

        @block.vector
        def _(dve):
            def mask(g):
                if isinstance(g, int) and g == 0:
                    dve.wait_ge(const_in, 16 * CONSTS)
                dve.wait_ge(adjS_in, g * 32 + 32)
                dve.tensor_tensor(adj_or[:], adjS_u8[:], eye2[:, 0:S].unsqueeze(1).to_broadcast([P, NG, S]),
                                  ALU.max).then_inc(or_ready, 1)

            dve.memset(b_diag[:], 0.0).then_inc(zeroed, 1)
            dve.memset(u_cols[:], 0.0).then_inc(zeroed, 1)
            for n, (w, raw) in enumerate(((Wq, raw_q), (Wk, raw_k), (Wv, raw_v), (Wo, raw_o))):
                dve.wait_ge(early_hi, n + 1)
                dve.tensor_tensor(w[1][:], raw[:], w[0][:].bitcast(F32), ALU.subtract).then_inc(weights_ready, 1)

            def b_layout(g):
                dve.wait_ge(zeroed, 2)
                dve.wait_ge(nat_in, 16 * 2)
                for hh in range(H2):
                    dve.tensor_copy(b_diag[:, :, hh, 32 * hh:32 * hh + 1], W_nat[:, :, hh, D:D + 1]).then_inc(b_placed, 1)

            def G_low(g):
                for n in range(H2 * DC):
                    hh, dc = n // DC, n % DC
                    part = slice(hh * D, hh * D + D)
                    dve.wait_ge(G_hi, n + 1)
                    dve.tensor_copy(u_cols[:, dc, 32 * hh:32 * hh + 1], bankB[n % BANKS][:, D:D + 1]).then_inc(U_placed, 1)
                    dve.tensor_tensor(G[1][:, dc, part], bankB[n % BANKS][:, 0:D], G[0][:, dc, part].bitcast(F32),
                                      ALU.subtract).then_inc(prod_read, 1)
                dve.wait_ge(U_placed, H2 * DC)
                dve.tensor_copy(U[0][:], u_cols[:]).then_inc(U_hi, 1)
                dve.wait_ge(U_hi, 1)
                dve.tensor_tensor(U[1][:], u_cols[:], U[0][:].bitcast(F32), ALU.subtract).then_inc(weights_ready, 1)

            def late(g):
                dve.wait_ge(prod_full, 2 * H2 * DC + 1)
                dve.tensor_copy(r_bias[:], bankB[0][:, 0:KC]).then_inc(prod_read, 1)
                dve.wait_ge(prod_full, 2 * H2 * DC + 2)
                dve.tensor_copy(s0[:], bankB[1][:, 0:1]).then_inc(prod_read, 1)
                for n, (w, raw) in enumerate(((Wt, raw_W), (Aw, raw_A), (FF, raw_fc), (G2, raw_g2))):
                    dve.wait_ge(late_hi, n + 1)
                    hi, lo = (t[:, :, 0:D] if w is FF else t[:] for t in w)
                    dve.tensor_tensor(lo, raw[:], hi.bitcast(F32), ALU.subtract).then_inc(weights_ready, 1)
                dve.wait_ge(rows_in, 16 * 3)

            def low(out, bank, hi, which, name, bias=0.0, op=ALU.add):
                take(dve.scalar_tensor_tensor(out=out, in0=bank, scalar=bias, in1=hi.bitcast(F32), op0=op,
                                              op1=ALU.subtract), which, name)

            def gate_weights(g):
                for c in range(DC):
                    bank = await_tile(dve, "A", f"hT{c}", -1)
                    hi, lo = (t[:, c, D:2 * D] for t in FF)
                    dve.tensor_copy(hi, bank[:, 0:D]).then_inc(FF_hi, 1)
                    dve.wait_ge(FF_hi, c + 1)
                    low(lo, bank[:, 0:D], hi, "A", f"hT{c}")

            def softmax_and_Wh(A, B):
                def shift(j):
                    bank = await_tile(dve, "A", f"score{j}", A)
                    view = bank[:].rearrange("p (b t) -> p b t", b=NG)
                    dve.tensor_reduce(mx[:, j, :], view, AX.X, ALU.max).then_inc(max_ready, 1)
                    dve.wait_ge(max_ready, A * JB + (j + 1))
                    take(dve.tensor_tensor(probs[:, j, :].rearrange("p (b t) -> p b t", b=NG), view,
                                           mx[:, j, :].unsqueeze(2).to_broadcast([P, NG, S]), ALU.subtract),
                         "A", f"score{j}")

                def total(j):
                    dve.wait_ge(exp_ready, A * JB + (j + 1))
                    dve.tensor_reduce(den[:, j, :], probs[:, j, :].rearrange("p (b t) -> p b t", b=NG), AX.X,
                                      ALU.add).then_inc(sum_ready, 1)
                    dve.wait_ge(sum_ready, A * JB + (j + 1))
                    dve.reciprocal(den[:, j, :], den[:, j, :]).then_inc(den_ready, 1)

                def Wh_out(p):
                    for name, dst, bias in (("WhL", Wh[:, p, 0:2 * D], bW_all[:, 0:2 * D]),
                                            ("WhR", Wh[:, p, 2 * D:4 * D], bW_all[:, 2 * D:4 * D])):
                        bank = await_tile(dve, "B", f"{name}{p}", B)
                        take(dve.tensor_tensor(dst, bank[:], bias, ALU.add), "B", f"{name}{p}")

                for f, n in ((shift, 0), (shift, 1), (shift, 2), (shift, 3), (total, 0), (Wh_out, 0),
                             (total, 1), (Wh_out, 1), (total, 2), (Wh_out, 2), (total, 3), (Wh_out, 3)):
                    if (B if f is Wh_out else A) is not None:
                        f(n)

            def adj_scores(g):
                def masked(p):
                    dve.wait_ge(tanh_ready, g * NP + (p + 1))
                    for b in range(2):
                        rows = slice(b * S, b * S + S)
                        dve.tensor_tensor(Abuf[rows, p, :, rows], edges[rows, p, :, :],
                                          adjT_u8[rows, p:p + 1, :].to_broadcast([S, H2, S]), ALU.mult) \
                           .then_inc(A_ready, 1)

                dve.wait_ge(s_ready, g * H2 + H2)
                dve.wait_ge(adjT_in, g * 16 + 16)
                for p in range(NP):
                    bank = await_tile(dve, "B", f"adjscore{p}", g)
                    for b in range(2):
                        rows = slice(b * S, b * S + S)
                        ins = dve.tensor_tensor(edges[rows, p, :, :],
                                                bank[rows, 0:H2 * S].rearrange("p (h n) -> p h n", h=H2),
                                                s_all[rows, :, p * P + b * S:p * P + b * S + S], ALU.add)
                    take(ins, "B", f"adjscore{p}")
                    if p > 0:
                        masked(p - 1)
                masked(NP - 1)

            def attention(g):
                for c in range(DC):
                    for b in range(2):
                        dve.wait_ge(at_hi_ready, g * 4 + (2 * c + b + 1))
                        bank = bank_of("A", f"attn{c}{b}")[:, 0:NP * S].rearrange("p (q s) -> p q s", q=NP)
                        low(of_graph(at_lo, c, b), bank, of_graph(at_hi, c, b), "A", f"attn{c}{b}", bias_v[:, c:c + 1])

            def cat_low(g):
                for n in range(KC):
                    dve.wait_ge(cat_hi_ready, g * KC + (n + 1))
                    low(cat_lo[:, n, :], bank_of("B", f"cat{n}")[:], cat_hi[:, n, :], "B", f"cat{n}", 0.0, ALU.max)

            def moments(g, src, stats, mv, stats_sem, mv_sem):
                for p in range(NP):
                    dve.bn_stats(stats[:, p, :], src[:, p, :]).then_inc(stats_sem, 1)
                dve.wait_ge(stats_sem, g * NP + NP)
                carried(dve)
                for p in range(NP):
                    dve.bn_aggr(mv[:, p, :], stats[:, p, :]).then_inc(mv_sem, 1)

            def residual(g):
                dve.wait_ge(xb_ready, g + 1)
                for t2 in range(2):
                    bank = await_tile(dve, "A", f"y{t2}", g)
                    part = y[:, 2 * t2:2 * t2 + 2, :]
                    take(dve.tensor_tensor(part, bank[:].rearrange("p (q d) -> p q d", q=2), part, ALU.add),
                         "A", f"y{t2}")
                for t2 in range(2):
                    await_taken(dve, "A", f"y{t2}", g)
                moments(g, y, stats1, mv1, stats1_ready, mv1_ready)

            def normed(g, dst, src, mv, rstd, rstd_sem, done_sem):
                dve.wait_ge(rstd_sem, g + 1)
                for p in range(NP):
                    dve.tensor_scalar(dst[:, p, :], src[:, p, :], mv[:, p, 0:1], rstd[:, p:p + 1], ALU.subtract,
                                      ALU.mult).then_inc(done_sem, 1)

            def h_a(g):
                for t2 in range(2):
                    part = slice(2 * t2, 2 * t2 + 2)
                    await_taken(dve, "B", f"ha{t2}", g)
                    dve.tensor_tensor(res[:, part, :], h[:, part, :], ha[:, part, :], ALU.add).then_inc(g_ready, 1)
                    dve.tensor_tensor(gate[:, part, 0:D], gate[:, part, 0:D], ha[:, part, :], ALU.subtract) \
                       .then_inc(g_ready, 1)

            def h_T(g):
                if not isinstance(g, int) or g > 0:
                    dve.wait_ge(g_ready, g * 4)
                normed(g, h, y, mv1, rstd1, rstd1_ready, h_ready)
                for c in range(DC):
                    dve.wait_ge(hT_hi_ready, g * DC + (c + 1))
                    low(hT_lo[:, c, :], bank_of("A", f"hT{c}")[:], hT_hi[:, c, :], "A", f"hT{c}")

            def ha_T(g):
                for c in range(DC):
                    dve.wait_ge(haT_hi_ready, g * DC + (c + 1))
                    low(haT_lo[:, c, :], bank_of("B", f"haT{c}")[:], haT_hi[:, c, :], "B", f"haT{c}")

            def gate_z(g):
                dve.wait_ge(gate_biased, g + 1)
                for t2 in range(2):
                    bank = await_tile(dve, "B", f"z{t2}", g)
                    part = gate[:, 2 * t2:2 * t2 + 2, D:2 * D]
                    take(dve.tensor_tensor(part, bank[:].rearrange("p (q d) -> p q d", q=2), part, ALU.add),
                         "B", f"z{t2}")

            def gated(g, t2):
                part = slice(2 * t2, 2 * t2 + 2)
                dve.wait_ge(gate_tanh, g * 2 + (t2 + 1))
                if t2 == 0:
                    dve.wait_ge(g_ready, g * 4 + 4)
                dve.scalar_tensor_tensor(out=gate[:, part, 0:D], in0=gate[:, part, D:2 * D], scalar=1.0,
                                         in1=gate[:, part, 0:D], op0=ALU.add, op1=ALU.mult).then_inc(e_ready, 1)
                dve.wait_ge(e_ready, g * 2 + (t2 + 1))
                dve.scalar_tensor_tensor(out=res[:, part, :], in0=gate[:, part, 0:D], scalar=0.5,
                                         in1=res[:, part, :], op0=ALU.mult, op1=ALU.add).then_inc(res_ready, 1)
                dve.wait_ge(res_ready, g * 2 + (t2 + 1))

            def norm(g):
                for t2 in range(2):
                    gated(g, t2)
                moments(g, res, stats2, mv2, stats2_ready, mv2_ready)
                normed(g, res, res, mv2, rstd2, rstd2_ready, out_ready)

            whole(dve, {("setup", "g1 fc"): gate_weights, ("S", "M1"): b_layout, ("S", "G"): G_low,
                        ("S", "r"): late,
                        ("L", "norm"): norm, ("N", "x"): mask, ("AB", "softmax"): softmax_and_Wh,
                        ("B", "adjscore"): adj_scores, ("A", "attn"): attention, ("B", "cat"): cat_low,
                        ("A", "y"): residual, ("B", "ha"): h_a, ("A", "hT"): h_T, ("B", "haT"): ha_T,
                        ("B", "z"): gate_z})

        @block.gpsimd
        def _(pool):
            pool.memset(half[:], -0.5).then_inc(consts_ready, 1)

            def x_low(g):
                pool.wait_ge(x_hi_ready, g + 1)
                pool.tensor_tensor(x_lo[:], x_raw[:], x_hi[:].bitcast(F32), ALU.subtract).then_inc(x_ready, 1)
                pool.wait_ge(or_ready, g + 1)
                carried(pool)
                pool.tensor_scalar(adj_or[:], adj_or[:], NEG, -NEG, ALU.mult, ALU.add).then_inc(mask_ready, 1)

            def hT_whole(g):
                for c in range(DC):
                    await_taken(pool, "A", f"hT{c}", g)
                if isinstance(g, int) and g == 0:
                    pool.wait_ge(prod_read, H2 * DC + 2)
                else:
                    await_tile(pool, "B", "ha1", g - 1)
                    carried(pool)
                pool.tensor_tensor(hT[:], hT_hi[:].bitcast(F32), hT_lo[:].bitcast(F32), ALU.add).then_inc(hT_ready, 1)

            def A_zeros(A, B):
                if A is not None and B is not None:
                    for j in range(JB):
                        await_tile(pool, "A", f"score{j}", A)
                    for b in range(2):
                        carried(pool)
                        pool.memset(Abuf[b * S:b * S + S, :, :, (1 - b) * S:(2 - b) * S], 0.0).then_inc(A_zeroed, 1)
                        pool.wait_ge(A_zeroed, B * 2 + (b + 1))

            def s_spread(g):
                await_taken(pool, "B", "s", g)
                if not isinstance(g, int) or g > 0:
                    pool.wait_ge(stored, g * 16)
                for hh in range(H2):
                    carried(pool)
                    pool.partition_broadcast(s_all[:, hh, :], s_row[32 * hh:32 * hh + 1, :]).then_inc(s_ready, 1)
                    pool.wait_ge(s_ready, g * H2 + (hh + 1))

            def probs_scaled(g):
                if isinstance(g, int) and g == 0:
                    pool.wait_ge(rows_in, 16 * 3)
                pool.wait_ge(x_in, g * 16 + 16)
                pool.tensor_tensor(y[:], y[:], bo_all[:, 0:D].unsqueeze(1).to_broadcast([P, NP, D]), ALU.add) \
                    .then_inc(xb_ready, 1)
                for j in range(JB):
                    pool.wait_ge(den_ready, g * JB + (j + 1))
                    view = probs[:, j, :].rearrange("p (b t) -> p b t", b=NG)
                    pool.tensor_tensor(view, view, den[:, j, :].unsqueeze(2).to_broadcast([P, NG, S]), ALU.mult) \
                        .then_inc(probs_ready, 1)

            def root(g, mv, rstd, mv_sem, var_sem, rstd_sem):
                pool.wait_ge(mv_sem, g * NP + NP)
                carried(pool)
                pool.tensor_scalar(rstd[:], mv[:, :, 1], EPS, None, ALU.add).then_inc(var_sem, 1)
                pool.wait_ge(var_sem, g + 1)
                pool.tensor_tensor(rstd[:], rstd[:], half[:], ALU.pow).then_inc(rstd_sem, 1)

            def gate_bias(g):
                if isinstance(g, int) and g == 0:
                    pool.wait_ge(rows_in, 16 * 3)
                for p in range(NP):
                    await_taken(pool, "B", f"gate{p}", g)
                part = gate[:, :, D:2 * D]
                pool.tensor_tensor(part, part, gb_all[:].unsqueeze(1).to_broadcast([P, NP, D]), ALU.add) \
                    .then_inc(gate_biased, 1)

            whole(pool, {("B", "cat"): gate_bias,("N", "x"): x_low, ("B", "T"): hT_whole, ("B", "s"): s_spread,
                         ("AB", "softmax"): A_zeros, ("A", "score"): probs_scaled,
                         ("A", "y"): lambda g: root(g, mv1, rstd1, mv1_ready, var1_ready, rstd1_ready),
                         ("L", "norm"): lambda g: root(g, mv2, rstd2, mv2_ready, var2_ready, rstd2_ready)})


def kernel(**inputs):
    import concourse.bacc as _bacc
    from concourse.bass_utils import run_bass_kernel_spmd as _run

    a = {k: np.asarray(t) for k, t in inputs.items()}
    x, adj = a["x"], a["adj"]

    def by_chunk(w):
        return w.reshape(-1, P, w.shape[-1]).transpose(1, 0, 2)

    def heads_first(w):
        return w.reshape(JB, 2, HD, -1).transpose(1, 0, 2, 3).reshape(D, -1)

    sq = np.arange(S)
    r, f = sq // 8, sq % 8
    dr, df = np.abs(r[:, None] - r[None]), np.abs(f[:, None] - f[None])
    diag = np.eye(S, dtype=bool)
    static = [df == 0, dr == 0, (r[:, None] - f[:, None]) == (r - f)[None], (r[:, None] + f[:, None]) == (r + f)[None],
              ((dr == 2) & (df == 1)) | ((dr == 1) & (df == 2)) | diag, (dr <= 1) & (df <= 1)]
    masks = np.where(np.stack(static), 0.0, -NEG).astype(np.float32)
    masks = masks.reshape(JB - 1, 2, S, S).transpose(1, 2, 0, 3).reshape(P, JB - 1, S)

    W, bW = a["L1_gnn_W"], a["L1_gnn_bW"]
    arrays = {
        "x": x.reshape(GROUPS, NP, P, D),
        "xT": x.reshape(GROUPS, TOK, DC, P).transpose(0, 3, 2, 1),
        "adjS": adj.reshape(GROUPS, NG, S, S).transpose(0, 2, 1, 3),
        "adjT": adj.reshape(GROUPS, NP, 2, S, S).transpose(0, 2, 4, 1, 3).reshape(GROUPS, P, NP, S),
        "masks": masks,
        "eye": np.eye(P, dtype=np.float32),
        "wq": by_chunk(heads_first(a["L0_gnn_Wq"]).T), "bq": heads_first(a["L0_gnn_bq"]).reshape(DC, P).T,
        "wk": by_chunk(heads_first(a["L0_gnn_Wk"]).T), "bk": heads_first(a["L0_gnn_bk"]).reshape(DC, P).T,
        "wv": by_chunk(heads_first(a["L0_gnn_Wv"]).T), "bv": heads_first(a["L0_gnn_bv"]).reshape(DC, P).T,
        "wo": by_chunk(heads_first(a["L0_gnn_Wo"].T)), "bo": a["L0_gnn_bo"].reshape(1, D),
        "Wn": np.concatenate([W, bW[:, :, None]], axis=2).reshape(H2, DC, P, D + 1).transpose(2, 1, 0, 3),
        "WT": by_chunk(W.transpose(2, 0, 1).reshape(D, H2 * D)),
        "bWrow": bW.reshape(1, H2 * D),
        "attn": a["L1_gnn_attn"].reshape(H2, DC, P, D).transpose(2, 1, 0, 3),
        "AwT": by_chunk(a["L1_gnn_A_w"].T),
        "fcn": by_chunk(a["L1_gnn_fc_w"]),
        "fcT": by_chunk(a["L1_gnn_fc_w"].T),
        "g1T": by_chunk(a["L1_gnn_g1_w"].T),
        "g2T": by_chunk(a["L1_gnn_g2_w"].T),
        "gb": a["L1_gnn_gbias"].reshape(1, D),
    }
    nc = _bacc.Bacc("TRN2", target_bir_lowering=False, num_devices=1)
    arrays = {k: np.ascontiguousarray(t) for k, t in arrays.items()}
    args = {k: nc.dram_tensor(f"in_{k}", t.shape, mybir.dt.from_np(t.dtype), kind="ExternalInput").ap()
            for k, t in arrays.items()}
    out = nc.dram_tensor("out_0", (GROUPS, NP, P, D), F32, kind="ExternalOutput").ap()
    stage_kernel(nc, out=out, **args)
    got = _run(nc, [{f"in_{k}": t for k, t in arrays.items()}], core_ids=[0])
    return got.results[0]["out_0"].reshape(GRAPHS, S, D)
```

```python
import numpy as np
import concourse.bass as bass
from concourse import mybir
from contextlib import ExitStack

F32 = mybir.dt.float32
F32R = mybir.dt.float32r
BF16 = mybir.dt.bfloat16
U8 = mybir.dt.uint8
ACT = mybir.ActivationFunctionType
ALU = mybir.AluOpType
AX = mybir.AxisListType

GRAPHS, S, D = 128, 64, 256
P = 128
HEADS, HD = 8, 32
H2 = 4
NG = 8
NP = NG // 2
TOK = NG * S
GROUPS = GRAPHS // NG
DC = D // P
JB = HEADS // 2
KC = H2 * DC
SCALE = float(1.0 / np.sqrt(HD))
NEG = 1.0e9
EPS = 1e-5
BANKS = 4

A_TILES = (["q0", "q1", "k0", "k1", "hT0", "hT1", "v0", "v1"]
           + [f"score{j}" for j in range(JB)] + [f"probT{j}" for j in range(JB)]
           + [f"attn{c}{b}" for c in range(DC) for b in range(2)] + ["y0", "y1"])
B_TILES = (["s"] + [f"T{n}" for n in range(KC)]
           + ["WhL0", "WhR0", "gate0"] + [f"adjscore{p}" for p in range(NP)]
           + [f"{k}{p}" for p in range(1, NP) for k in ("WhL", "WhR", "gate")] + [f"cat{n}" for n in range(KC)]
           + ["ha0", "ha1", "haT0", "haT1", "z0", "z1"])


def stage_kernel(nc, x, xT, adjS, adjT, masks, eye, wq, bq, wk, bk, wv, bv, wo, bo,
                 Wn, WT, bWrow, attn, AwT, fcn, fcT, g1T, g2T, gb, out):
    ctx = ExitStack()
    with ctx:
        def sem(name):
            return ctx.enter_context(nc.semaphore(name))

        place = [0]

        def at(name, shape, dt, offset):
            return nc.alloc_sbuf_tensor_at(name, shape, dt, offset=offset)

        def size(shape, dt):
            n = 4 if dt in (F32, F32R) else 2 if dt == BF16 else 1
            for s in shape[1:]:
                n *= s
            return (n + 31) // 32 * 32

        base = (nc.sbuf_base + 31) // 32 * 32

        def region(nbytes):
            off = base + place[0]
            place[0] += (nbytes + 31) // 32 * 32
            return off

        def sb(name, shape, dt=F32):
            return at(name, shape, dt, region(size(shape, dt)))

        def pair(name, shape):
            return sb(name + "_hi", shape, F32R), sb(name + "_lo", shape, F32R)

        Wq, Wk, Wv, Wo = (pair(n, [P, DC, D]) for n in ("wq", "wk", "wv", "wo"))
        Wt = pair("wt", [P, DC, H2 * D])
        G = pair("g", [P, DC, H2 * D])
        FF = pair("ff", [P, DC, 2 * D])
        Aw = pair("aw", [P, KC, D])
        G2 = pair("g2", [P, DC, D])
        U = pair("u", [P, DC, P])
        bias_q, bias_k, bias_v = (sb(n, [P, DC]) for n in ("bias_q", "bias_k", "bias_v"))
        r_bias = sb("r_bias", [P, KC])
        s0 = sb("s0", [P, 1])
        bW_all = sb("bW_all", [P, H2 * D])
        bo_all = sb("bo_all", [P, D])
        gb_all = sb("gb_all", [P, D])
        ident = sb("ident", [P, P])
        mask_static = sb("mask_static", [P, JB - 1, S], BF16)
        eye2 = sb("eye2", [P, S])
        half = sb("half", [P, NP])

        r_x, r_qk, r_S, r_PT = region(8192), region(8192), region(8192), region(8192)
        r_T, r_Wh, r_gate, r_s = region(32768), region(16384), region(8192), region(8192)
        x_hi = at("x_hi", [P, DC, TOK], F32R, r_x)
        x_lo = at("x_lo", [P, DC, TOK], F32R, r_x + 4096)
        qT = at("qT", [P, DC, TOK], F32, r_qk)
        kT = at("kT", [P, DC, TOK], F32, r_qk + 4096)
        Abuf = at("Abuf", [P, NP, H2, P], F32, r_qk)
        probs = at("probs", [P, JB, TOK], F32, r_S)
        at_hi = at("at_hi", [P, DC, TOK], F32R, r_S)
        at_lo = at("at_lo", [P, DC, TOK], F32R, r_S + 4096)
        haT_hi = at("haT_hi", [P, DC, TOK], F32R, r_S)
        haT_lo = at("haT_lo", [P, DC, TOK], F32R, r_S + 4096)
        PT = at("PT", [P, JB, NP, P], F32, r_PT)
        x_raw = at("x_raw", [P, DC, TOK], F32, r_PT)
        s_row = at("s_row", [P, TOK], F32, r_PT + 4096)
        T = at("T", [P, DC, H2, TOK], F32, r_T + 16384)
        hT = at("hT", [P, DC, TOK], F32, r_T)
        edges = at("edges", [P, NP, H2, S], F32, r_T + 4096)
        cat_hi = at("cat_hi", [P, KC, TOK], F32R, r_T)
        cat_lo = at("cat_lo", [P, KC, TOK], F32R, r_T + 16384)
        Wh = at("Wh", [P, NP, H2 * D], F32, r_Wh)
        gate = at("gate", [P, NP, 2 * D], F32, r_gate)
        s_all = at("s_all", [P, H2, TOK], F32, r_s)
        ha = at("ha", [P, NP, D], F32, r_s)
        res = at("res", [P, NP, D], F32, r_s + 4096)
        v = sb("v", [P, NP, D])
        y = sb("y", [P, NP, D])
        h = sb("h", [P, NP, D])
        hT_hi, hT_lo = pair("hT", [P, DC, TOK])
        adjS_u8 = sb("adjS_u8", [P, NG, S], U8)
        adj_or = sb("adj_or", [P, NG, S], BF16)
        mask_dyn = adj_or
        adjT_u8 = sb("adjT_u8", [P, NP, S], U8)
        mx = sb("mx", [P, JB, NG])
        den = sb("den", [P, JB, NG])
        stats1 = sb("stats1", [P, NP, 6])
        mv1 = sb("mv1", [P, NP, 2])
        rstd1 = sb("rstd1", [P, NP])
        stats2 = sb("stats2", [P, NP, 6])
        mv2 = sb("mv2", [P, NP, 2])
        rstd2 = sb("rstd2", [P, NP])
        W_nat = at("W_nat", [P, DC, H2, D + 1], F32, r_T)
        attn_nat = at("attn_nat", [P, DC, H2, D], F32, r_T + 8256)
        M1 = at("M1", [P, DC, H2, D + 1], F32, r_T + 16448)
        fc_nat = at("fc_nat", [P, DC, D], F32, r_T + 24704)
        g1_raw = at("g1_raw", [P, DC, D], F32, r_T + 26752)
        r_rows = at("r_rows", [P, D + 1], F32, r_s)
        u_cols = at("u_cols", [P, DC, P], F32, r_T + 28800)
        raw_q, raw_k, raw_v, raw_o = (at(n, [P, DC, D], F32, r_S + 2048 * i)
                                      for i, n in enumerate(("raw_q", "raw_k", "raw_v", "raw_o")))
        raw_W = at("raw_W", [P, DC, H2 * D], F32, r_Wh)
        raw_A = at("raw_A", [P, KC, D], F32, r_Wh + 8192)
        raw_fc = at("raw_fc", [P, DC, D], F32, r_gate)
        raw_g2 = at("raw_g2", [P, DC, D], F32, r_gate + 2048)
        raw_m = at("raw_m", [P, JB - 1, S], F32, r_gate + 4096)
        assert base + place[0] <= nc.sbuf_usable_end, (base, place[0], nc.sbuf_usable_end)

        bankA = [ctx.enter_context(nc.psum_tensor(f"bankA{b}", [P, 512], F32)) for b in range(BANKS)]
        bankB = [ctx.enter_context(nc.psum_tensor(f"bankB{b}", [P, 512], F32)) for b in range(BANKS)]

        fullA, takenA, fullB, takenB = ([sem(f"{n}{b}") for b in range(BANKS)]
                                        for n in ("fullA", "takenA", "fullB", "takenB"))
        early_in = [sem(f"early_in{n}") for n in range(4)]
        nat_in, late_in, const_in, gate_in, rows_in = (
            sem(n) for n in ("nat_in", "late_in", "const_in", "gate_in", "rows_in"))
        xT_in, x_in, adjS_in, adjT_in, stored = (sem(n) for n in ("xT_in", "x_in", "adjS_in", "adjT_in", "stored"))
        early_hi, late_hi, weights_ready, zeroed, prod_full, prod_read, r_placed, consts_ready = (
            sem(n) for n in ("early_hi", "late_hi", "weights_ready", "zeroed", "prod_full", "prod_read",
                             "r_placed", "consts_ready"))
        M1_ready, G_hi, FF_hi, U_placed, U_hi = (sem(n) for n in ("M1_ready", "G_hi", "FF_hi", "U_placed", "U_hi"))
        x_hi_ready, x_ready, or_ready, mask_ready, xb_ready = (
            sem(n) for n in ("x_hi_ready", "x_ready", "or_ready", "mask_ready", "xb_ready"))
        max_ready, shifted, exp_ready, sum_ready, den_ready, probs_ready = (
            sem(n) for n in ("max_ready", "shifted", "exp_ready", "sum_ready", "den_ready", "probs_ready"))
        at_hi_ready, stats1_ready, mv1_ready, var1_ready, rstd1_ready, h_ready, hT_hi_ready = (
            sem(n) for n in ("at_hi_ready", "stats1_ready", "mv1_ready", "var1_ready", "rstd1_ready",
                             "h_ready", "hT_hi_ready"))
        A_zeroed, gate_biased, h_kept = sem("A_zeroed"), sem("gate_biased"), sem("h_kept")
        s_ready, hT_ready, tanh_ready, A_ready, cat_hi_ready, haT_hi_ready, g_ready, gate_tanh = (
            sem(n) for n in ("s_ready", "hT_ready", "tanh_ready", "A_ready", "cat_hi_ready",
                             "haT_hi_ready", "g_ready", "gate_tanh"))
        e_ready, res_ready, stats2_ready, mv2_ready, var2_ready, rstd2_ready, out_ready = (
            sem(n) for n in ("e_ready", "res_ready", "stats2_ready", "mv2_ready", "var2_ready",
                             "rstd2_ready", "out_ready"))

        def spot(tiles, name):
            n = tiles.index(name)
            return n % BANKS, n // BANKS, len(tiles[n % BANKS::BANKS])

        def before(which, name, g):
            b, u, n = spot(TILES[which], name)
            if name in ("hT0", "hT1"):
                if isinstance(g, int) and g == GROUPS - 1:
                    return b, n * GROUPS
                g = g + 1
            return b, g * n + u

        TILES = {"A": A_TILES, "B": B_TILES}
        BANK = {"A": bankA, "B": bankB}
        FULL = {"A": fullA, "B": fullB}
        TAKEN = {"A": takenA, "B": takenB}

        def bank_of(which, name):
            return BANK[which][spot(TILES[which], name)[0]]

        def claim(pe, which, name, g):
            b, count = before(which, name, g)
            if not isinstance(count, int) or count > 0:
                pe.wait_ge(TAKEN[which][b], count)
            return BANK[which][b]

        def filled(ins, which, name):
            ins.then_inc(FULL[which][spot(TILES[which], name)[0]], 1)

        def await_tile(eng, which, name, g):
            b, count = before(which, name, g)
            eng.wait_ge(FULL[which][b], count + 1)
            return BANK[which][b]

        def take(ins, which, name):
            ins.then_inc(TAKEN[which][spot(TILES[which], name)[0]], 1)

        def await_taken(eng, which, name, g):
            b, count = before(which, name, g)
            eng.wait_ge(TAKEN[which][b], count + 1)

        def steps(A, B, more, run):
            for stage, step in (("AB", "T and score"), ("B", "T"), ("L", "norm"), ("B", "s"), ("AB", "softmax"),
                                ("A", "score"), ("B", "adjscore"), ("S", "M1"), ("AB", "Wh and probT"),
                                ("A", "attn"), ("S", "G"), ("B", "cat"), ("N", "x"), ("A", "y"), ("S", "r"),
                                ("B", "keep h"), ("A", "h"), ("B", "ha"), ("N", "qk"), ("A", "hT"), ("S", "late"),
                                ("B", "haT"), ("N", "v"), ("B", "z")):
                if (stage, step) not in run:
                    continue
                if stage == "AB":
                    run[stage, step](A, B)
                    continue
                g = {"A": A, "B": B, "N": A + 1 if more else None, "S": 0 if B is None and more else None,
                     "L": None if B is None or (isinstance(B, int) and B == 0) else B - 1}[stage]
                if g is not None:
                    run[stage, step](g)

        def whole(eng, run):
            for first in (("N", "x"), ("N", "qk"), ("setup", "g1 fc"), ("N", "v")):
                if first in run:
                    run[first](0)
            steps(0, None, True, run)
            steps(1, 0, True, run)
            with eng.Fori(2, GROUPS - 1) as i:
                steps(i, i - 1, True, run)
            steps(GROUPS - 1, GROUPS - 2, False, run)
            steps(None, GROUPS - 1, False, run)
            if ("L", "norm") in run:
                run["L", "norm"](GROUPS - 1)

        CONSTS = 7

        passed = sem("passed")

        def carried(eng):
            eng.sem_inc(passed, 1)

        def of_graph(t, c, b):
            return t[:, c, :].rearrange("p (q b s) -> p q b s", q=NP, b=2)[:, :, b, :]

        block = ctx.enter_context(nc.Block())

        @block.sync
        def _(sp):
            def load(dst, src, s):
                sp.dma_start(dst, src).then_inc(s, 16)

            def xT_load(g):
                load(x_raw[:], xT[bass.ds(g, 1)].rearrange("o p c t -> (o p) c t"), xT_in)

            def adjS_load(g):
                for half_ in range(2):
                    load(adjS_u8[half_ * S:half_ * S + S], adjS[bass.ds(g, 1)].rearrange("o s b t -> (o s) b t"), adjS_in)

            def x_load(g):
                load(y[:], x[bass.ds(g, 1)].rearrange("o p t d -> t (o p) d"), x_in)

            load(raw_q[:], wq, early_in[0])
            xT_load(0)
            load(raw_k[:], wk, early_in[1])
            for dst, src in ((bias_q, bq), (bias_k, bk), (bias_v, bv), (ident, eye)):
                load(dst[:], src, const_in)
            load(raw_m[:], masks, const_in)
            for half_ in range(2):
                load(eye2[half_ * S:half_ * S + S], eye[0:S, 0:S], const_in)
            load(fc_nat[:], fcn, gate_in)
            load(g1_raw[:], g1T, gate_in)
            load(raw_v[:], wv, early_in[2])
            adjS_load(0)
            load(raw_o[:], wo, early_in[3])
            load(W_nat[:], Wn, nat_in)
            load(attn_nat[:], attn, nat_in)
            x_load(0)
            for dst, src, n in ((bo_all, bo, D), (bW_all, bWrow, H2 * D), (gb_all, gb, D)):
                load(dst[:], src.to_broadcast([P, n]), rows_in)
            load(raw_W[:], WT, late_in)
            load(raw_A[:], AwT, late_in)
            load(raw_fc[:], fcT, late_in)
            load(raw_g2[:], g2T, late_in)

            def adjT_load(g):
                if not isinstance(g, int) or g > 0:
                    sp.wait_ge(A_ready, g * NP * 2)
                    carried(sp)
                load(adjT_u8[:], adjT[bass.ds(g, 1)].rearrange("o m p n -> (o m) p n"), adjT_in)

            def next_loads(g):
                for c in range(DC):
                    for b in range(2):
                        await_taken(sp, "A", f"attn{c}{b}", g - 1)
                carried(sp)
                xT_load(g)
                sp.wait_ge(or_ready, g)
                carried(sp)
                adjS_load(g)

            def x_next(g):
                sp.wait_ge(h_ready, g * NP)
                carried(sp)
                x_load(g)

            def store(g):
                sp.wait_ge(out_ready, g * NP + NP)
                carried(sp)
                sp.dma_start(out[bass.ds(g, 1)].rearrange("o p t d -> t (o p) d"), res[:]).then_inc(stored, 16)

            def turn(A, B, more):
                if B is not None:
                    adjT_load(B)
                    if not isinstance(B, int) or B > 0:
                        store(B - 1)
                if more:
                    next_loads(A + 1)
                    x_next(A + 1)

            turn(0, None, True)
            turn(1, 0, True)
            with sp.Fori(2, GROUPS - 1) as i:
                turn(i, i - 1, True)
            turn(GROUPS - 1, GROUPS - 2, False)
            turn(None, GROUPS - 1, False)
            store(GROUPS - 1)
            sp.wait_ge(stored, 16 * GROUPS)

        @block.tensor
        def _(pe):
            def product(out, a, b, asel, bsel, first, last):
                pe.matmul(out, asel(a[0]), bsel(b[1]), start=first, stop=False)
                pe.matmul(out, asel(a[1]), bsel(b[0]), start=False, stop=False)
                return pe.matmul(out, asel(a[0]), bsel(b[0]), start=False, stop=last)

            def dense(out, terms):
                for n, (a, b, asel, bsel) in enumerate(terms):
                    ins = product(out, a, b, asel, bsel, n == 0, n == len(terms) - 1)
                return ins

            def M1_products(g):
                pe.wait_ge(nat_in, 16 * 2)
                for n in range(H2 * DC):
                    hh, pc = n // DC, n % DC
                    if n >= BANKS:
                        pe.wait_ge(M1_ready, n - BANKS + 1)
                    for oc in range(DC):
                        ins = pe.matmul(bankB[n % BANKS][:, 0:D + 1], attn_nat[:, oc, hh, pc * P:pc * P + P],
                                        W_nat[:, oc, hh, :], start=oc == 0, stop=oc == DC - 1)
                    ins.then_inc(prod_full, 1)

            def G_products(g):
                pe.wait_ge(M1_ready, H2 * DC)
                for n in range(H2 * DC):
                    hh, dc = n // DC, n % DC
                    if n >= BANKS:
                        pe.wait_ge(prod_read, n - BANKS + 1)
                    for pc in range(DC):
                        ins = pe.matmul(bankB[n % BANKS][:, 0:D + 1], M1[:, pc, hh, dc * P:dc * P + P],
                                        W_nat[:, pc, hh, :], start=pc == 0, stop=pc == DC - 1)
                    ins.then_inc(prod_full, 1)
                pe.wait_ge(prod_read, H2 * DC - BANKS + 1)
                for hh in range(H2):
                    for pc in range(DC):
                        ins = pe.matmul(bankB[0][32 * hh:32 * hh + 1, 0:D + 1], M1[:, pc, hh, D:D + 1],
                                        W_nat[:, pc, hh, :], start=pc == 0, stop=pc == DC - 1)
                ins.then_inc(prod_full, 1)

            def r_columns(g):
                pe.wait_ge(r_placed, H2)
                for c in range(DC):
                    ins = pe.transpose(bankB[c][:, 0:P], r_rows[:, c * P:c * P + P], ident[:])
                    ins.then_inc(prod_full, 1)

            end = filled

            def qk(g):
                pe.wait_ge(x_ready, g + 1)
                for i, (n, w) in enumerate((("q", Wq), ("k", Wk))):
                    if isinstance(g, int) and g == 0:
                        pe.wait_ge(weights_ready, i + 1)
                    for c in range(DC):
                        claim(pe, "A", f"{n}{c}", g)
                        end(dense(bank_of("A", f"{n}{c}")[:], [
                            (w, (x_hi, x_lo), lambda t, k=k: t[:, k, c * P:c * P + P], lambda t, k=k: t[:, k, :])
                            for k in range(DC)]), "A", f"{n}{c}")

            def values(g):
                if isinstance(g, int) and g == 0:
                    pe.wait_ge(weights_ready, 3)
                for t2 in range(2):
                    claim(pe, "A", f"v{t2}", g)
                    for q in range(2):
                        p = 2 * t2 + q
                        ins = dense(bank_of("A", f"v{t2}")[:, q * D:q * D + D], [
                            ((x_hi, x_lo), Wv, lambda t, k=k: t[:, k, p * P:p * P + P], lambda t, k=k: t[:, k, :])
                            for k in range(DC)])
                    end(ins, "A", f"v{t2}")

            def scores(g, banks, graphs):
                if 0 in banks and 0 in graphs:
                    for n in ("q0", "q1", "k0", "k1"):
                        await_taken(pe, "A", n, g)
                if 0 in graphs:
                    for j in banks:
                        claim(pe, "A", f"score{j}", g)
                for b in graphs:
                    for c in range(DC):
                        for j in banks:
                            rows = slice(HD * j, HD * j + HD)
                            ins = pe.matmul(bank_of("A", f"score{j}")[c * S:c * S + S, b * S:b * S + S],
                                            qT[rows, c, b * S:b * S + S], kT[rows, c, b * S:b * S + S],
                                            start=True, stop=True)
                            if b == NG - 1 and c == DC - 1:
                                end(ins, "A", f"score{j}")

            def probs_T(g):
                for j in range(JB):
                    pe.wait_ge(probs_ready, g * JB + (j + 1))
                    claim(pe, "A", f"probT{j}", g)
                    for p in range(NP):
                        ins = pe.transpose(bank_of("A", f"probT{j}")[:, p * P:p * P + P], probs[:, j, p * P:p * P + P], ident[:])
                    end(ins, "A", f"probT{j}")

            def attention(g):
                for j in range(JB):
                    await_taken(pe, "A", f"probT{j}", g)
                for t2 in range(2):
                    await_taken(pe, "A", f"v{t2}", g)
                for c in range(DC):
                    for b in range(2):
                        claim(pe, "A", f"attn{c}{b}", g)
                    carried(pe)
                    for p in range(NP):
                        for j in range(JB):
                            for b in range(2):
                                ins = pe.matmul(bank_of("A", f"attn{c}{b}")[HD * j:HD * j + HD, p * S:p * S + S],
                                                v[b * S:b * S + S, p, c * P + HD * j:c * P + HD * j + HD],
                                                PT[b * S:b * S + S, j, p, c * S:c * S + S], start=True, stop=True)
                                if p == NP - 1 and j == JB - 1:
                                    end(ins, "A", f"attn{c}{b}")

            def project(g):
                if isinstance(g, int) and g == 0:
                    pe.wait_ge(weights_ready, 4)
                for c in range(DC):
                    for b in range(2):
                        await_taken(pe, "A", f"attn{c}{b}", g)
                for t2 in range(2):
                    claim(pe, "A", f"y{t2}", g)
                    for q in range(2):
                        p = 2 * t2 + q
                        ins = dense(bank_of("A", f"y{t2}")[:, q * D:q * D + D], [
                            ((at_hi, at_lo), Wo, lambda t, k=k: t[:, k, p * P:p * P + P], lambda t, k=k: t[:, k, :])
                            for k in range(DC)])
                    end(ins, "A", f"y{t2}")

            def transposed(src, which, names):
                for c in range(DC):
                    claim(pe, which, names[c], names[2])
                    for p in range(NP):
                        ins = pe.transpose(bank_of(which, names[c])[:, p * P:p * P + P], src[:, p, c * P:c * P + P], ident[:])
                    end(ins, which, names[c])

            def gate_weights(g):
                pe.wait_ge(gate_in, 16 * 2)
                for c in range(DC):
                    bank = claim(pe, "A", f"hT{c}", -1)
                    for oc in range(DC):
                        ins = pe.matmul(bank[:, 0:D], fc_nat[:, oc, c * P:c * P + P], g1_raw[:, oc, :],
                                        start=oc == 0, stop=oc == DC - 1)
                    filled(ins, "A", f"hT{c}")

            def h_T(g):
                pe.wait_ge(h_ready, g * NP + NP)
                transposed(h, "A", ("hT0", "hT1", g))

            SCORES_FROM = 3

            def s_rows(g):
                if isinstance(g, int) and g == 0:
                    pe.wait_ge(prod_read, H2 * DC + 3)
                    pe.wait_ge(weights_ready, 5)
                for c in range(DC):
                    await_taken(pe, "A", f"hT{c}", g)
                claim(pe, "B", "s", g)
                end(dense(bank_of("B", "s")[:], [
                    (U, (hT_hi, hT_lo), lambda t, k=k: t[:, k, :], lambda t, k=k: t[:, k, :])
                    for k in range(DC)]), "B", "s")

            def T_tile(g, n):
                claim(pe, "B", f"T{n}", g)
                end(dense(bank_of("B", f"T{n}")[:], [
                    (G, (hT_hi, hT_lo), lambda t, k=k: t[:, k, n * P:n * P + P], lambda t, k=k: t[:, k, :])
                    for k in range(DC)]), "B", f"T{n}")

            def T_and_scores(A, B):
                if B is not None:
                    s_rows(B)
                for n in range(KC):
                    if B is not None:
                        T_tile(B, n)
                    if A is not None and 0 <= n - SCORES_FROM < 4:
                        two, part = (n - SCORES_FROM) // 2 * 2, (n - SCORES_FROM) % 2 * (NG // 2)
                        scores(A, range(two, two + 2), range(part, part + NG // 2))

            def W_h(g, pairs):
                if isinstance(g, int) and g == 0:
                    pe.wait_ge(weights_ready, 9)
                for p in pairs:
                    for name, w, off in (("WhL", Wt, 0), ("WhR", Wt, 2 * D), ("gate", FF, 0)):
                        claim(pe, "B", f"{name}{p}", g)
                        end(dense(bank_of("B", f"{name}{p}")[:], [
                            ((hT_hi, hT_lo), w, lambda t, k=k: t[:, k, p * P:p * P + P],
                             lambda t, k=k: t[:, k, off:off + 2 * D]) for k in range(DC)]), "B", f"{name}{p}")

            def W_h_and_probs_T(A, B):
                if B is not None:
                    W_h(B, range(1, NP - 1))
                if A is not None:
                    probs_T(A)
                if B is not None:
                    W_h(B, range(NP - 1, NP))

            def adj_scores(g):
                W_h(g, range(1))
                for n in range(KC - BANKS, KC):
                    await_taken(pe, "B", f"T{n}", g)
                pe.wait_ge(hT_ready, g + 1)
                for p in range(NP):
                    bank = claim(pe, "B", f"adjscore{p}", g)
                    for k in range(DC):
                        for b in range(2):
                            graph = slice(p * P + b * S, p * P + b * S + S)
                            ins = pe.matmul(bank[b * S:b * S + S, 0:H2 * S].rearrange("p (h n) -> p h n", h=H2),
                                            hT[:, k, graph], T[:, k, :, graph], start=k == 0, stop=k == DC - 1)
                    end(ins, "B", f"adjscore{p}")

            def cat(g):
                for name in ("WhL2", "WhR2", "WhL3", "WhR3"):
                    await_taken(pe, "B", name, g)
                pe.wait_ge(A_ready, g * NP * 2 + NP * 2)
                pe.wait_ge(A_zeroed, 2 * g if isinstance(g, int) and g == GROUPS - 1 else g * 2 + 2)
                for n in range(KC):
                    claim(pe, "B", f"cat{n}", g)
                    for p in range(NP):
                        ins = pe.matmul(bank_of("B", f"cat{n}")[:, p * P:p * P + P], Wh[:, p, n * P:n * P + P],
                                        Abuf[:, p, n // DC, :], start=True, stop=True)
                    end(ins, "B", f"cat{n}")

            def h_a(g):
                for t2 in range(2):
                    claim(pe, "B", f"ha{t2}", g)
                    for q in range(2):
                        p = 2 * t2 + q
                        for k in range(KC):
                            if p == 0:
                                await_taken(pe, "B", f"cat{k}", g)
                            ins = product(bank_of("B", f"ha{t2}")[:, q * D:q * D + D], (cat_hi, cat_lo), Aw,
                                          lambda t: t[:, k, p * P:p * P + P], lambda t: t[:, k, :], k == 0, k == KC - 1)
                    end(ins, "B", f"ha{t2}")

            def ha_T(g):
                for t2 in range(2):
                    await_taken(pe, "B", f"ha{t2}", g)
                transposed(ha, "B", ("haT0", "haT1", g))

            def gate_z(g):
                for c in range(DC):
                    await_taken(pe, "B", f"haT{c}", g)
                for t2 in range(2):
                    claim(pe, "B", f"z{t2}", g)
                    for q in range(2):
                        p = 2 * t2 + q
                        ins = dense(bank_of("B", f"z{t2}")[:, q * D:q * D + D], [
                            ((haT_hi, haT_lo), G2, lambda t, k=k: t[:, k, p * P:p * P + P], lambda t, k=k: t[:, k, :])
                            for k in range(DC)])
                    end(ins, "B", f"z{t2}")

            whole(pe, {("setup", "g1 fc"): gate_weights, ("S", "M1"): M1_products, ("S", "G"): G_products,
                       ("S", "r"): r_columns, ("N", "qk"): qk, ("N", "v"): values, ("AB", "T and score"): T_and_scores,
                       ("A", "attn"): attention, ("A", "y"): project, ("A", "hT"): h_T,
                       ("AB", "Wh and probT"): W_h_and_probs_T, ("B", "adjscore"): adj_scores, ("B", "cat"): cat,
                       ("B", "ha"): h_a, ("B", "haT"): ha_T, ("B", "z"): gate_z})

        @block.scalar
        def _(act):
            def x_split(g):
                act.wait_ge(xT_in, g * 16 + 16)
                act.activation(x_hi[:], x_raw[:], ACT.Copy).then_inc(x_hi_ready, 1)

            for n, (w, raw) in enumerate(((Wq, raw_q), (Wk, raw_k), (Wv, raw_v), (Wo, raw_o))):
                act.wait_ge(early_in[n], 16)
                act.activation(w[0][:], raw[:], ACT.Copy).then_inc(early_hi, 1)
                if n == 0:
                    x_split(0)
                if n == 1:
                    act.wait_ge(const_in, 16 * CONSTS)
                    act.activation(mask_static[:], raw_m[:], ACT.Copy).then_inc(consts_ready, 1)

            def late(g):
                act.wait_ge(late_in, 16 * 4)
                for w, raw in ((Wt[0][:], raw_W), (Aw[0][:], raw_A), (FF[0][:, :, 0:D], raw_fc), (G2[0][:], raw_g2)):
                    act.activation(w, raw[:], ACT.Copy).then_inc(late_hi, 1)

            def qk(g):
                for n, dst, bias in (("q", qT, bias_q), ("k", kT, bias_k)):
                    for c in range(DC):
                        bank = await_tile(act, "A", f"{n}{c}", g)
                        take(act.activation(dst[:, c, :], bank[:], ACT.Identity, bias=bias[:, c:c + 1]),
                             "A", f"{n}{c}")

            def values(g):
                for t2 in range(2):
                    bank = await_tile(act, "A", f"v{t2}", g)
                    take(act.activation(v[:, 2 * t2:2 * t2 + 2, :], bank[:].rearrange("p (q d) -> p q d", q=2),
                                        ACT.Copy), "A", f"v{t2}")

            def exps(g):
                for j in range(JB):
                    act.wait_ge(shifted, g * JB + (j + 1))
                    act.activation(probs[:, j, :], probs[:, j, :], ACT.Exp, scale=SCALE).then_inc(exp_ready, 1)

            def probs_T(g):
                for j in range(JB):
                    bank = await_tile(act, "A", f"probT{j}", g)
                    take(act.activation(PT[:, j, :, :], bank[:].rearrange("p (q s) -> p q s", q=NP), ACT.Copy),
                         "A", f"probT{j}")

            def attention(g):
                for c in range(DC):
                    for b in range(2):
                        bank = await_tile(act, "A", f"attn{c}{b}", g)
                        act.activation(of_graph(at_hi, c, b), bank[:, 0:NP * S].rearrange("p (q s) -> p q s", q=NP),
                                       ACT.Identity, bias=bias_v[:, c:c + 1]).then_inc(at_hi_ready, 1)

            def h_T(g):
                for c in range(DC):
                    bank = await_tile(act, "A", f"hT{c}", g)
                    act.activation(hT_hi[:, c, :], bank[:], ACT.Copy).then_inc(hT_hi_ready, 1)

            def T_and_s(g):
                bank = await_tile(act, "B", "s", g)
                if not isinstance(g, int) or g > 0:
                    act.wait_ge(s_ready, g * H2)
                take(act.activation(s_row[:], bank[:], ACT.Identity, bias=s0[:, 0:1]), "B", "s")
                for n in range(KC):
                    bank = await_tile(act, "B", f"T{n}", g)
                    take(act.activation(T[:, n % DC, n // DC, :], bank[:], ACT.Identity, bias=r_bias[:, n:n + 1]),
                         "B", f"T{n}")

            def W_h(g, pairs):
                if 0 in pairs and (not isinstance(g, int) or g > 0):
                    act.wait_ge(res_ready, g * 2)
                for p in pairs:
                    bank = await_tile(act, "B", f"gate{p}", g)
                    take(act.activation(gate[:, p, :], bank[:], ACT.Copy), "B", f"gate{p}")

            def W_h_and_probs_T(A, B):
                if B is not None:
                    W_h(B, range(1, NP - 1))
                if A is not None:
                    probs_T(A)
                if B is not None:
                    W_h(B, range(NP - 1, NP))

            def adj_scores(g):
                W_h(g, range(1))
                for p in range(NP):
                    await_taken(act, "B", f"adjscore{p}", g)
                    act.activation(edges[:, p, :, :], edges[:, p, :, :], ACT.Tanh).then_inc(tanh_ready, 1)

            def cat(g):
                for n in range(KC):
                    bank = await_tile(act, "B", f"cat{n}", g)
                    act.activation(cat_hi[:, n, :], bank[:], ACT.Relu).then_inc(cat_hi_ready, 1)

            def keep_h(g):
                act.wait_ge(A_ready, g * NP * 2 + NP * 2)
                act.activation(res[:], h[:], ACT.Copy).then_inc(h_kept, 1)

            def h_a(g):
                for t2 in range(2):
                    bank = await_tile(act, "B", f"ha{t2}", g)
                    take(act.activation(ha[:, 2 * t2:2 * t2 + 2, :], bank[:].rearrange("p (q d) -> p q d", q=2),
                                        ACT.Copy), "B", f"ha{t2}")

            def ha_T(g):
                for c in range(DC):
                    bank = await_tile(act, "B", f"haT{c}", g)
                    act.activation(haT_hi[:, c, :], bank[:], ACT.Copy).then_inc(haT_hi_ready, 1)

            def gate_z(g):
                for t2 in range(2):
                    await_taken(act, "B", f"z{t2}", g)
                    part = gate[:, 2 * t2:2 * t2 + 2, D:2 * D]
                    act.activation(part, part, ACT.Tanh, scale=0.5).then_inc(gate_tanh, 1)

            def M1_copies(g):
                for n in range(H2 * DC):
                    act.wait_ge(prod_full, n + 1)
                    act.activation(M1[:, n % DC, n // DC, :], bankB[n % BANKS][:, 0:D + 1], ACT.Copy) \
                       .then_inc(M1_ready, 1)

            def G_high(g):
                for n in range(H2 * DC):
                    act.wait_ge(prod_full, H2 * DC + n + 1)
                    hh, dc = n // DC, n % DC
                    act.activation(G[0][:, dc, hh * D:hh * D + D], bankB[n % BANKS][:, 0:D], ACT.Copy) \
                       .then_inc(G_hi, 1)

            def later_x_split(g):
                if not isinstance(g, int) or g > 0:
                    x_split(g)

            whole(act, {("N", "x"): later_x_split, ("S", "M1"): M1_copies, ("S", "G"): G_high,
                        ("S", "r"): late, ("N", "qk"): qk, ("N", "v"): values, ("A", "score"): exps,
                        ("AB", "Wh and probT"): W_h_and_probs_T, ("A", "attn"): attention, ("A", "hT"): h_T,
                        ("B", "T"): T_and_s, ("B", "adjscore"): adj_scores, ("B", "cat"): cat,
                        ("B", "keep h"): keep_h, ("B", "ha"): h_a, ("B", "haT"): ha_T, ("B", "z"): gate_z})

        @block.vector
        def _(dve):
            def mask(g):
                if isinstance(g, int) and g == 0:
                    dve.wait_ge(const_in, 16 * CONSTS)
                dve.wait_ge(adjS_in, g * 32 + 32)
                dve.tensor_tensor(adj_or[:], adjS_u8[:], eye2[:, 0:S].unsqueeze(1).to_broadcast([P, NG, S]),
                                  ALU.max).then_inc(or_ready, 1)

            dve.memset(r_rows[:], 0.0).then_inc(zeroed, 1)
            dve.memset(u_cols[:], 0.0).then_inc(zeroed, 1)
            for n, (w, raw) in enumerate(((Wq, raw_q), (Wk, raw_k), (Wv, raw_v), (Wo, raw_o))):
                dve.wait_ge(early_hi, n + 1)
                dve.tensor_tensor(w[1][:], raw[:], w[0][:].bitcast(F32), ALU.subtract).then_inc(weights_ready, 1)
                if n == 0:
                    dve.wait_ge(x_hi_ready, 1)
                    dve.tensor_tensor(x_lo[:], x_raw[:], x_hi[:].bitcast(F32), ALU.subtract).then_inc(x_ready, 1)

            def G_low(g):
                for n in range(H2 * DC):
                    hh, dc = n // DC, n % DC
                    part = slice(hh * D, hh * D + D)
                    dve.wait_ge(G_hi, n + 1)
                    dve.tensor_copy(u_cols[:, dc, 32 * hh:32 * hh + 1], bankB[n % BANKS][:, D:D + 1]).then_inc(U_placed, 1)
                    dve.tensor_tensor(G[1][:, dc, part], bankB[n % BANKS][:, 0:D], G[0][:, dc, part].bitcast(F32),
                                      ALU.subtract).then_inc(prod_read, 1)
                dve.wait_ge(prod_full, 2 * H2 * DC + 1)
                dve.wait_ge(zeroed, 2)
                for hh in range(H2):
                    row = slice(32 * hh, 32 * hh + 1)
                    dve.tensor_copy(r_rows[row, :], bankB[0][row, 0:D + 1]).then_inc(r_placed, 1)
                dve.wait_ge(U_placed, H2 * DC)
                dve.tensor_copy(U[0][:], u_cols[:]).then_inc(U_hi, 1)
                dve.wait_ge(U_hi, 1)
                dve.tensor_tensor(U[1][:], u_cols[:], U[0][:].bitcast(F32), ALU.subtract).then_inc(weights_ready, 1)

            def r_out(g):
                dve.wait_ge(r_placed, H2)
                dve.tensor_copy(s0[:], r_rows[:, D:D + 1]).then_inc(prod_read, 1)
                columns = r_bias[:].rearrange("p (h c) -> p h c", h=H2)
                for c in range(DC):
                    dve.wait_ge(prod_full, 2 * H2 * DC + 1 + (c + 1))
                    dve.tensor_copy(columns[:, :, c:c + 1],
                                    bankB[c][:, 0:P].rearrange("p (h r) -> p h r", h=H2)[:, :, 0:1]) \
                       .then_inc(prod_read, 1)

            def late(g):
                for n, (w, raw) in enumerate(((Wt, raw_W), (Aw, raw_A), (FF, raw_fc), (G2, raw_g2))):
                    dve.wait_ge(late_hi, n + 1)
                    hi, lo = (t[:, :, 0:D] if w is FF else t[:] for t in w)
                    dve.tensor_tensor(lo, raw[:], hi.bitcast(F32), ALU.subtract).then_inc(weights_ready, 1)
                dve.wait_ge(rows_in, 16 * 3)

            def low(out, bank, hi, which, name, bias=0.0, op=ALU.add):
                take(dve.scalar_tensor_tensor(out=out, in0=bank, scalar=bias, in1=hi.bitcast(F32), op0=op,
                                              op1=ALU.subtract), which, name)

            def gate_weights(g):
                for c in range(DC):
                    bank = await_tile(dve, "A", f"hT{c}", -1)
                    hi, lo = (t[:, c, D:2 * D] for t in FF)
                    dve.tensor_copy(hi, bank[:, 0:D]).then_inc(FF_hi, 1)
                    dve.wait_ge(FF_hi, c + 1)
                    low(lo, bank[:, 0:D], hi, "A", f"hT{c}")

            def softmax_and_edges(A, B):
                def shift(j):
                    bank = await_tile(dve, "A", f"score{j}", A)
                    if j == 0 and isinstance(A, int) and A == 0:
                        dve.wait_ge(consts_ready, 2)
                    if j == JB - 1:
                        dve.wait_ge(mask_ready, A + 1)
                    m = mask_dyn[:] if j == JB - 1 else mask_static[:, j:j + 1, :].to_broadcast([P, NG, S])
                    view = probs[:, j, :].rearrange("p (b t) -> p b t", b=NG)
                    take(dve.tensor_tensor(view, bank[:].rearrange("p (b t) -> p b t", b=NG), m, ALU.add),
                         "A", f"score{j}")
                    await_taken(dve, "A", f"score{j}", A)
                    dve.tensor_reduce(mx[:, j, :], view, AX.X, ALU.max).then_inc(max_ready, 1)
                    dve.wait_ge(max_ready, A * JB + (j + 1))
                    dve.tensor_tensor(view, view, mx[:, j, :].unsqueeze(2).to_broadcast([P, NG, S]), ALU.subtract) \
                       .then_inc(shifted, 1)

                def total(j):
                    dve.wait_ge(exp_ready, A * JB + (j + 1))
                    dve.tensor_reduce(den[:, j, :], probs[:, j, :].rearrange("p (b t) -> p b t", b=NG), AX.X,
                                      ALU.add).then_inc(sum_ready, 1)
                    dve.wait_ge(sum_ready, A * JB + (j + 1))
                    dve.reciprocal(den[:, j, :], den[:, j, :]).then_inc(den_ready, 1)

                def Wh_out(p):
                    for name, dst, bias in (("WhL", Wh[:, p, 0:2 * D], bW_all[:, 0:2 * D]),
                                            ("WhR", Wh[:, p, 2 * D:4 * D], bW_all[:, 2 * D:4 * D])):
                        bank = await_tile(dve, "B", f"{name}{p}", B)
                        take(dve.tensor_tensor(dst, bank[:], bias, ALU.add), "B", f"{name}{p}")

                def plus_s(p):
                    if p == 0:
                        dve.wait_ge(s_ready, B * H2 + H2)
                    bank = await_tile(dve, "B", f"adjscore{p}", B)
                    for b in range(2):
                        rows = slice(b * S, b * S + S)
                        ins = dve.tensor_tensor(edges[rows, p, :, :],
                                                bank[rows, 0:H2 * S].rearrange("p (h n) -> p h n", h=H2),
                                                s_all[rows, :, p * P + b * S:p * P + b * S + S], ALU.add)
                    take(ins, "B", f"adjscore{p}")

                def masked(p):
                    if p == 0:
                        dve.wait_ge(adjT_in, B * 16 + 16)
                    dve.wait_ge(tanh_ready, B * NP + (p + 1))
                    for b in range(2):
                        rows = slice(b * S, b * S + S)
                        dve.tensor_tensor(Abuf[rows, p, :, rows], edges[rows, p, :, :],
                                          adjT_u8[rows, p:p + 1, :].to_broadcast([S, H2, S]), ALU.mult) \
                           .then_inc(A_ready, 1)

                for f, n in ((shift, 0), (shift, 1), (shift, 2), (shift, 3), (Wh_out, 0), (total, 0), (plus_s, 0),
                             (plus_s, 1), (masked, 0), (plus_s, 2), (total, 1), (masked, 1), (plus_s, 3), (total, 2),
                             (masked, 2), (Wh_out, 1), (total, 3), (masked, 3), (Wh_out, 2), (Wh_out, 3)):
                    if (A if f in (shift, total) else B) is not None:
                        f(n)

            def attention(g):
                for c in range(DC):
                    for b in range(2):
                        dve.wait_ge(at_hi_ready, g * 4 + (2 * c + b + 1))
                        bank = bank_of("A", f"attn{c}{b}")[:, 0:NP * S].rearrange("p (q s) -> p q s", q=NP)
                        low(of_graph(at_lo, c, b), bank, of_graph(at_hi, c, b), "A", f"attn{c}{b}", bias_v[:, c:c + 1])

            def cat_low(g):
                for n in range(KC):
                    dve.wait_ge(cat_hi_ready, g * KC + (n + 1))
                    low(cat_lo[:, n, :], bank_of("B", f"cat{n}")[:], cat_hi[:, n, :], "B", f"cat{n}", 0.0, ALU.max)

            def moments(g, src, stats, mv, stats_sem, mv_sem):
                for p in range(NP):
                    dve.bn_stats(stats[:, p, :], src[:, p, :]).then_inc(stats_sem, 1)
                dve.wait_ge(stats_sem, g * NP + NP)
                carried(dve)
                for p in range(NP):
                    dve.bn_aggr(mv[:, p, :], stats[:, p, :]).then_inc(mv_sem, 1)

            def residual(g):
                dve.wait_ge(xb_ready, g + 1)
                for t2 in range(2):
                    bank = await_tile(dve, "A", f"y{t2}", g)
                    part = y[:, 2 * t2:2 * t2 + 2, :]
                    take(dve.tensor_tensor(part, bank[:].rearrange("p (q d) -> p q d", q=2), part, ALU.add),
                         "A", f"y{t2}")
                for t2 in range(2):
                    await_taken(dve, "A", f"y{t2}", g)
                moments(g, y, stats1, mv1, stats1_ready, mv1_ready)

            def normed(g, dst, src, mv, rstd, rstd_sem, done_sem):
                dve.wait_ge(rstd_sem, g + 1)
                for p in range(NP):
                    dve.tensor_scalar(dst[:, p, :], src[:, p, :], mv[:, p, 0:1], rstd[:, p:p + 1], ALU.subtract,
                                      ALU.mult).then_inc(done_sem, 1)

            def h_a(g):
                dve.wait_ge(h_kept, g + 1)
                for t2 in range(2):
                    part = slice(2 * t2, 2 * t2 + 2)
                    await_taken(dve, "B", f"ha{t2}", g)
                    dve.tensor_tensor(res[:, part, :], res[:, part, :], ha[:, part, :], ALU.add).then_inc(g_ready, 1)
                    dve.tensor_tensor(gate[:, part, 0:D], gate[:, part, 0:D], ha[:, part, :], ALU.subtract) \
                       .then_inc(g_ready, 1)

            def new_h(g):
                if not isinstance(g, int) or g > 0:
                    dve.wait_ge(h_kept, g)
                normed(g, h, y, mv1, rstd1, rstd1_ready, h_ready)

            def h_T(g):
                for c in range(DC):
                    dve.wait_ge(hT_hi_ready, g * DC + (c + 1))
                    low(hT_lo[:, c, :], bank_of("A", f"hT{c}")[:], hT_hi[:, c, :], "A", f"hT{c}")

            def ha_T(g):
                for c in range(DC):
                    dve.wait_ge(haT_hi_ready, g * DC + (c + 1))
                    low(haT_lo[:, c, :], bank_of("B", f"haT{c}")[:], haT_hi[:, c, :], "B", f"haT{c}")

            def gate_z(g):
                dve.wait_ge(gate_biased, g + 1)
                for t2 in range(2):
                    bank = await_tile(dve, "B", f"z{t2}", g)
                    part = gate[:, 2 * t2:2 * t2 + 2, D:2 * D]
                    take(dve.tensor_tensor(part, bank[:].rearrange("p (q d) -> p q d", q=2), part, ALU.add),
                         "B", f"z{t2}")

            def gated(g, t2):
                part = slice(2 * t2, 2 * t2 + 2)
                dve.wait_ge(gate_tanh, g * 2 + (t2 + 1))
                if t2 == 0:
                    dve.wait_ge(g_ready, g * 4 + 4)
                dve.scalar_tensor_tensor(out=gate[:, part, 0:D], in0=gate[:, part, D:2 * D], scalar=1.0,
                                         in1=gate[:, part, 0:D], op0=ALU.add, op1=ALU.mult).then_inc(e_ready, 1)
                dve.wait_ge(e_ready, g * 2 + (t2 + 1))
                dve.scalar_tensor_tensor(out=res[:, part, :], in0=gate[:, part, 0:D], scalar=0.5,
                                         in1=res[:, part, :], op0=ALU.mult, op1=ALU.add).then_inc(res_ready, 1)
                dve.wait_ge(res_ready, g * 2 + (t2 + 1))

            def norm(g):
                for t2 in range(2):
                    gated(g, t2)
                moments(g, res, stats2, mv2, stats2_ready, mv2_ready)
                normed(g, res, res, mv2, rstd2, rstd2_ready, out_ready)

            whole(dve, {("setup", "g1 fc"): gate_weights, ("S", "G"): G_low,
                        ("S", "r"): r_out, ("S", "late"): late,
                        ("L", "norm"): norm, ("N", "x"): mask, ("AB", "softmax"): softmax_and_edges,
                        ("A", "attn"): attention, ("B", "cat"): cat_low,
                        ("A", "y"): residual, ("B", "ha"): h_a, ("A", "h"): new_h, ("A", "hT"): h_T, ("B", "haT"): ha_T,
                        ("B", "z"): gate_z})

        @block.gpsimd
        def _(pool):
            pool.memset(half[:], -0.5).then_inc(consts_ready, 1)

            def x_low(g):
                if not isinstance(g, int) or g > 0:
                    pool.wait_ge(x_hi_ready, g + 1)
                    pool.tensor_tensor(x_lo[:], x_raw[:], x_hi[:].bitcast(F32), ALU.subtract).then_inc(x_ready, 1)
                pool.wait_ge(or_ready, g + 1)
                carried(pool)
                pool.tensor_scalar(adj_or[:], adj_or[:], NEG, -NEG, ALU.mult, ALU.add).then_inc(mask_ready, 1)

            def hT_whole(g):
                for c in range(DC):
                    await_taken(pool, "A", f"hT{c}", g)
                if isinstance(g, int) and g == 0:
                    pool.wait_ge(prod_read, H2 * DC + 3)
                else:
                    await_tile(pool, "B", "ha1", g - 1)
                    carried(pool)
                pool.tensor_tensor(hT[:], hT_hi[:].bitcast(F32), hT_lo[:].bitcast(F32), ALU.add).then_inc(hT_ready, 1)

            def A_zeros(A, B):
                if A is not None and B is not None:
                    for j in range(JB):
                        await_tile(pool, "A", f"score{j}", A)
                    for b in range(2):
                        carried(pool)
                        pool.memset(Abuf[b * S:b * S + S, :, :, (1 - b) * S:(2 - b) * S], 0.0).then_inc(A_zeroed, 1)
                        pool.wait_ge(A_zeroed, B * 2 + (b + 1))

            def s_spread(g):
                await_taken(pool, "B", "s", g)
                if not isinstance(g, int) or g > 0:
                    pool.wait_ge(stored, g * 16)
                for hh in range(H2):
                    carried(pool)
                    pool.partition_broadcast(s_all[:, hh, :], s_row[32 * hh:32 * hh + 1, :]).then_inc(s_ready, 1)
                    pool.wait_ge(s_ready, g * H2 + (hh + 1))

            def probs_scaled(g):
                if isinstance(g, int) and g == 0:
                    pool.wait_ge(rows_in, 16 * 3)
                pool.wait_ge(x_in, g * 16 + 16)
                pool.tensor_tensor(y[:], y[:], bo_all[:, 0:D].unsqueeze(1).to_broadcast([P, NP, D]), ALU.add) \
                    .then_inc(xb_ready, 1)
                for j in range(JB):
                    pool.wait_ge(den_ready, g * JB + (j + 1))
                    view = probs[:, j, :].rearrange("p (b t) -> p b t", b=NG)
                    pool.tensor_tensor(view, view, den[:, j, :].unsqueeze(2).to_broadcast([P, NG, S]), ALU.mult) \
                        .then_inc(probs_ready, 1)

            def root(g, mv, rstd, mv_sem, var_sem, rstd_sem):
                pool.wait_ge(mv_sem, g * NP + NP)
                carried(pool)
                pool.tensor_scalar(rstd[:], mv[:, :, 1], EPS, None, ALU.add).then_inc(var_sem, 1)
                pool.wait_ge(var_sem, g + 1)
                pool.tensor_tensor(rstd[:], rstd[:], half[:], ALU.pow).then_inc(rstd_sem, 1)

            def gate_bias(g):
                if isinstance(g, int) and g == 0:
                    pool.wait_ge(rows_in, 16 * 3)
                for p in range(NP):
                    await_taken(pool, "B", f"gate{p}", g)
                part = gate[:, :, D:2 * D]
                pool.tensor_tensor(part, part, gb_all[:].unsqueeze(1).to_broadcast([P, NP, D]), ALU.add) \
                    .then_inc(gate_biased, 1)

            whole(pool, {("B", "cat"): gate_bias,("N", "x"): x_low, ("B", "T"): hT_whole, ("B", "s"): s_spread,
                         ("AB", "softmax"): A_zeros, ("A", "score"): probs_scaled,
                         ("A", "y"): lambda g: root(g, mv1, rstd1, mv1_ready, var1_ready, rstd1_ready),
                         ("L", "norm"): lambda g: root(g, mv2, rstd2, mv2_ready, var2_ready, rstd2_ready)})


def kernel(**inputs):
    import concourse.bacc as _bacc
    from concourse.bass_utils import run_bass_kernel_spmd as _run

    a = {k: np.asarray(t) for k, t in inputs.items()}
    x, adj = a["x"], a["adj"]

    def by_chunk(w):
        return w.reshape(-1, P, w.shape[-1]).transpose(1, 0, 2)

    def heads_first(w):
        return w.reshape(JB, 2, HD, -1).transpose(1, 0, 2, 3).reshape(D, -1)

    sq = np.arange(S)
    r, f = sq // 8, sq % 8
    dr, df = np.abs(r[:, None] - r[None]), np.abs(f[:, None] - f[None])
    diag = np.eye(S, dtype=bool)
    static = [df == 0, dr == 0, (r[:, None] - f[:, None]) == (r - f)[None], (r[:, None] + f[:, None]) == (r + f)[None],
              ((dr == 2) & (df == 1)) | ((dr == 1) & (df == 2)) | diag, (dr <= 1) & (df <= 1)]
    masks = np.where(np.stack(static), 0.0, -NEG).astype(np.float32)
    masks = masks.reshape(JB - 1, 2, S, S).transpose(1, 2, 0, 3).reshape(P, JB - 1, S)

    W, bW = a["L1_gnn_W"], a["L1_gnn_bW"]
    arrays = {
        "x": x.reshape(GROUPS, NP, P, D),
        "xT": x.reshape(GROUPS, TOK, DC, P).transpose(0, 3, 2, 1),
        "adjS": adj.reshape(GROUPS, NG, S, S).transpose(0, 2, 1, 3),
        "adjT": adj.reshape(GROUPS, NP, 2, S, S).transpose(0, 2, 4, 1, 3).reshape(GROUPS, P, NP, S),
        "masks": masks,
        "eye": np.eye(P, dtype=np.float32),
        "wq": by_chunk(heads_first(a["L0_gnn_Wq"]).T), "bq": heads_first(a["L0_gnn_bq"]).reshape(DC, P).T,
        "wk": by_chunk(heads_first(a["L0_gnn_Wk"]).T), "bk": heads_first(a["L0_gnn_bk"]).reshape(DC, P).T,
        "wv": by_chunk(heads_first(a["L0_gnn_Wv"]).T), "bv": heads_first(a["L0_gnn_bv"]).reshape(DC, P).T,
        "wo": by_chunk(heads_first(a["L0_gnn_Wo"].T)), "bo": a["L0_gnn_bo"].reshape(1, D),
        "Wn": np.concatenate([W, bW[:, :, None]], axis=2).reshape(H2, DC, P, D + 1).transpose(2, 1, 0, 3),
        "WT": by_chunk(W.transpose(2, 0, 1).reshape(D, H2 * D)),
        "bWrow": bW.reshape(1, H2 * D),
        "attn": a["L1_gnn_attn"].reshape(H2, DC, P, D).transpose(2, 1, 0, 3),
        "AwT": by_chunk(a["L1_gnn_A_w"].T),
        "fcn": by_chunk(a["L1_gnn_fc_w"]),
        "fcT": by_chunk(a["L1_gnn_fc_w"].T),
        "g1T": by_chunk(a["L1_gnn_g1_w"].T),
        "g2T": by_chunk(a["L1_gnn_g2_w"].T),
        "gb": a["L1_gnn_gbias"].reshape(1, D),
    }
    nc = _bacc.Bacc("TRN2", target_bir_lowering=False, num_devices=1)
    arrays = {k: np.ascontiguousarray(t) for k, t in arrays.items()}
    args = {k: nc.dram_tensor(f"in_{k}", t.shape, mybir.dt.from_np(t.dtype), kind="ExternalInput").ap()
            for k, t in arrays.items()}
    out = nc.dram_tensor("out_0", (GROUPS, NP, P, D), F32, kind="ExternalOutput").ap()
    stage_kernel(nc, out=out, **args)
    got = _run(nc, [{f"in_{k}": t for k, t in arrays.items()}], core_ids=[0])
    return got.results[0]["out_0"].reshape(GRAPHS, S, D)
```
